# Optimizing a Trainium2 kernel written in Bass

```python
import numpy as np
import jax
import jax.numpy as jnp

def _softmax(x, axis=-1):
    return jax.nn.softmax(x, axis=axis)

def _gelu(x):
    return jax.nn.gelu(x, approximate=True)

def _silu(x):
    return jax.nn.silu(x)

def _sigmoid(x):
    return jax.nn.sigmoid(x)

def _layernorm(x, axis=-1, eps=1e-05):
    m = jnp.mean(x, axis=axis, keepdims=True)
    v = jnp.var(x, axis=axis, keepdims=True)
    return (x - m) / jnp.sqrt(v + eps)

def _scatter_add(tgt, idx, src, axis=0):
    return tgt.at[idx].add(src)

def _segment_sum(src, seg, n):
    return jax.ops.segment_sum(src, seg, n)
kernel_name = 'mk_sandwich_d2_jaxref_r8_ad9cd8'

def setup_inputs(seed: int=0):
    np.random.seed(seed)
    _w = jnp.asarray

    def _L0_attn_setup():
        import jax, jax.numpy as jnp
        import numpy as np
        B, S, E, H = (4, 512, 128, 16)
        D = E // H

        def _phi(x):
            return jax.nn.elu(x) + 1.0
        key = jax.random.key(seed)
        k1, k2, k3 = jax.random.split(key, 3)
        x = jax.random.normal(k1, (B, S, E), dtype=jnp.float32)
        W_qkv = jax.random.normal(k2, (E, 3 * E), dtype=jnp.float32) * E ** (-0.5)
        b_qkv = jnp.zeros((3 * E,), dtype=jnp.float32)
        W_proj = jax.random.normal(k3, (E, E), dtype=jnp.float32) * E ** (-0.5)
        b_proj = jnp.zeros((E,), dtype=jnp.float32)
        return {'x': x, 'W_qkv': W_qkv, 'b_qkv': b_qkv, 'W_proj': W_proj, 'b_proj': b_proj}
    _L0_attn_in = _L0_attn_setup()

    def _L0_ffn_setup():
        import jax, jax.numpy as jnp
        import numpy as np
        B, S, D_MODEL, D_FF, E, R, TOP_K = (4, 256, 128, 512, 8, 16, 2)
        key = jax.random.key(seed)
        ks = jax.random.split(key, 9)
        sd = 1.0 / np.sqrt(D_MODEL)
        return {'hidden_states': jax.random.normal(ks[0], (B, S, D_MODEL), jnp.float32), 'wi': jax.random.normal(ks[1], (D_FF, D_MODEL), jnp.float32) * sd, 'bi': jax.random.normal(ks[2], (D_FF,), jnp.float32) * 0.01, 'wo': jax.random.normal(ks[3], (D_MODEL, D_FF), jnp.float32) * (1.0 / np.sqrt(D_FF)), 'bo': jax.random.normal(ks[4], (D_MODEL,), jnp.float32) * 0.01, 'lora_A': jax.random.normal(ks[5], (E, R, D_MODEL), jnp.float32) * sd, 'lora_B': jax.random.normal(ks[6], (E, D_FF, R), jnp.float32) * 0.02, 'gate_w': jax.random.normal(ks[7], (E, D_MODEL), jnp.float32) * sd, 'gate_b': jax.random.normal(ks[8], (E,), jnp.float32) * 0.01}
    _L0_ffn_in = _L0_ffn_setup()

    def _L1_attn_setup():
        import jax, jax.numpy as jnp
        import numpy as np
        B, N, DIM = (2, 256, 128)
        H, DH = (16, 64)
        M = 16
        K = 64
        SCALE = DH ** (-0.5)
        NEG_INF = -jnp.inf
        key = jax.random.key(seed)
        ks = jax.random.split(key, 9)
        s = 0.02
        return {'x': jax.random.normal(ks[0], (B, N, DIM), jnp.float32), 'Wq': jax.random.normal(ks[1], (DIM, H * DH), jnp.float32) * s, 'Wkv': jax.random.normal(ks[2], (DIM, 2 * H * DH), jnp.float32) * s, 'Wo': jax.random.normal(ks[3], (H * DH, DIM), jnp.float32) * s, 'bo': jnp.zeros((DIM,), jnp.float32), 'pre_proj': jax.random.normal(ks[4], (H, H), jnp.float32), 'post_proj': jax.random.normal(ks[5], (H, H), jnp.float32), 'mem_k': jax.random.normal(ks[6], (H, M, DH), jnp.float32), 'mem_v': jax.random.normal(ks[7], (H, M, DH), jnp.float32)}
    _L1_attn_in = _L1_attn_setup()

    def _L1_ffn_setup():
        import jax, jax.numpy as jnp
        import numpy as np
        H = 128
        I = 256
        E = 8
        B, S = (2, 512)
        EPS = 1e-05
        INIT = 0.02

        def _layernorm(x, w, b):
            mu = jnp.mean(x, axis=-1, keepdims=True)
            var = jnp.mean(jnp.square(x - mu), axis=-1, keepdims=True)
            return (x - mu) * jax.lax.rsqrt(var + EPS) * w + b
        key = jax.random.key(seed)
        ks = jax.random.split(key, 9)
        return {'hidden_states': jax.random.normal(ks[0], (B, S, H), jnp.float32), 'ln_w': jnp.ones((H,), jnp.float32), 'ln_b': jnp.zeros((H,), jnp.float32), 'router_w': jax.random.normal(ks[1], (H, E), jnp.float32) * INIT, 'gate_w': jax.random.normal(ks[2], (E, H, I), jnp.float32) * INIT, 'up_w': jax.random.normal(ks[3], (E, H, I), jnp.float32) * INIT, 'down_w': jax.random.normal(ks[4], (E, I, H), jnp.float32) * INIT, 'sh_gate': jax.random.normal(ks[5], (H, I), jnp.float32) * INIT, 'sh_up': jax.random.normal(ks[6], (H, I), jnp.float32) * INIT, 'sh_down': jax.random.normal(ks[7], (I, H), jnp.float32) * INIT}
    _L1_ffn_in = _L1_ffn_setup()
    _d = {'L0_attn_x': _L0_attn_in['x'], 'L0_attn_W_qkv': _L0_attn_in['W_qkv'], 'L0_attn_b_qkv': _L0_attn_in['b_qkv'], 'L0_attn_W_proj': _L0_attn_in['W_proj'], 'L0_attn_b_proj': _L0_attn_in['b_proj'], 'L0_ffn_wi': _L0_ffn_in['wi'], 'L0_ffn_bi': _L0_ffn_in['bi'], 'L0_ffn_wo': _L0_ffn_in['wo'], 'L0_ffn_bo': _L0_ffn_in['bo'], 'L0_ffn_lora_A': _L0_ffn_in['lora_A'], 'L0_ffn_lora_B': _L0_ffn_in['lora_B'], 'L0_ffn_gate_w': _L0_ffn_in['gate_w'], 'L0_ffn_gate_b': _L0_ffn_in['gate_b'], 'L1_attn_Wq': _L1_attn_in['Wq'], 'L1_attn_Wkv': _L1_attn_in['Wkv'], 'L1_attn_Wo': _L1_attn_in['Wo'], 'L1_attn_bo': _L1_attn_in['bo'], 'L1_attn_pre_proj': _L1_attn_in['pre_proj'], 'L1_attn_post_proj': _L1_attn_in['post_proj'], 'L1_attn_mem_k': _L1_attn_in['mem_k'], 'L1_attn_mem_v': _L1_attn_in['mem_v'], 'L1_ffn_ln_w': _L1_ffn_in['ln_w'], 'L1_ffn_ln_b': _L1_ffn_in['ln_b'], 'L1_ffn_router_w': _L1_ffn_in['router_w'], 'L1_ffn_gate_w': _L1_ffn_in['gate_w'], 'L1_ffn_up_w': _L1_ffn_in['up_w'], 'L1_ffn_down_w': _L1_ffn_in['down_w'], 'L1_ffn_sh_gate': _L1_ffn_in['sh_gate'], 'L1_ffn_sh_up': _L1_ffn_in['sh_up'], 'L1_ffn_sh_down': _L1_ffn_in['sh_down']}
    _x0 = _d['L0_attn_x']
    _d['L0_attn_x'] = jax.random.normal(jax.random.fold_in(jax.random.key(seed), 1), (1, 2048, 128), dtype=_x0.dtype)
    del _x0
    return _d

def reference(L0_attn_x, L0_attn_W_qkv, L0_attn_b_qkv, L0_attn_W_proj, L0_attn_b_proj, L0_ffn_wi, L0_ffn_bi, L0_ffn_wo, L0_ffn_bo, L0_ffn_lora_A, L0_ffn_lora_B, L0_ffn_gate_w, L0_ffn_gate_b, L1_attn_Wq, L1_attn_Wkv, L1_attn_Wo, L1_attn_bo, L1_attn_pre_proj, L1_attn_post_proj, L1_attn_mem_k, L1_attn_mem_v, L1_ffn_ln_w, L1_ffn_ln_b, L1_ffn_router_w, L1_ffn_gate_w, L1_ffn_up_w, L1_ffn_down_w, L1_ffn_sh_gate, L1_ffn_sh_up, L1_ffn_sh_down):

    def _L0_attn_ref(x, W_qkv, b_qkv, W_proj, b_proj):
        import jax, jax.numpy as jnp
        import numpy as np
        B, S, E, H = (4, 512, 128, 16)
        D = E // H

        def _phi(x):
            return jax.nn.elu(x) + 1.0
        b, s, _ = x.shape
        qkv = (x @ W_qkv + b_qkv).reshape(b, s, 3, H, D)
        q, k, v = (qkv[:, :, 0], qkv[:, :, 1], qkv[:, :, 2])
        pq, pk = (_phi(q), _phi(k))
        kv = jnp.einsum('bshd,bshm->bhmd', pk, v)
        z = 1.0 / (jnp.einsum('bshd,bhd->bsh', pq, pk.sum(axis=1)) + 1e-06)
        attn = jnp.einsum('bshd,bhmd,bsh->bshm', pq, kv, z)
        attn = attn.reshape(b, s, H * D)
        _proj = attn @ W_proj + b_proj
        return attn

    def _L0_ffn_ref(hidden_states, wi, bi, wo, bo, lora_A, lora_B, gate_w, gate_b):
        import jax, jax.numpy as jnp
        import numpy as np
        B, S, D_MODEL, D_FF, E, R, TOP_K = (4, 256, 128, 512, 8, 16, 2)
        logits = jnp.einsum('bsd,ed->bse', hidden_states, gate_w) + gate_b
        scores = jax.nn.softmax(logits, axis=-1)
        top_v, top_i = jax.lax.top_k(scores, TOP_K)
        val_sum = top_v.sum(axis=-1)
        out = jnp.zeros_like(hidden_states)
        for e in range(E):
            count = (top_i == e).sum(axis=-1).astype(hidden_states.dtype)
            gate = count * val_sum
            inter = jnp.einsum('bsd,fd->bsf', hidden_states, wi) + bi + jnp.einsum('bsr,fr->bsf', jnp.einsum('bsd,rd->bsr', hidden_states, lora_A[e]), lora_B[e])
            h = jax.nn.relu(inter)
            expert_out = jnp.einsum('bsf,df->bsd', h, wo) + bo
            out = out + gate[..., None] * expert_out
        return out

    def _L1_attn_ref(x, Wq, Wkv, Wo, bo, pre_proj, post_proj, mem_k, mem_v):
        import jax, jax.numpy as jnp
        import numpy as np
        B, N, DIM = (2, 256, 128)
        H, DH = (16, 64)
        M = 16
        K = 64
        SCALE = DH ** (-0.5)
        NEG_INF = -jnp.inf
        b, n, _ = x.shape
        q = (x @ Wq).reshape(b, n, H, DH).transpose(0, 2, 1, 3)
        kv = x @ Wkv
        k, v = jnp.split(kv, 2, axis=-1)
        k = k.reshape(b, n, H, DH).transpose(0, 2, 1, 3)
        v = v.reshape(b, n, H, DH).transpose(0, 2, 1, 3)
        k = jnp.concatenate([jnp.broadcast_to(mem_k, (b, H, M, DH)), k], axis=2)
        v = jnp.concatenate([jnp.broadcast_to(mem_v, (b, H, M, DH)), v], axis=2)
        j = n + M
        dots = jnp.einsum('bhid,bhjd->bhij', q, k) * SCALE
        dots = jnp.einsum('bhij,hk->bkij', dots, pre_proj)
        causal = jnp.triu(jnp.ones((n, j), bool), j - n + 1)
        dots = jnp.where(causal, NEG_INF, dots)
        topk_vals = jax.lax.top_k(dots, K)[0]
        thresh = topk_vals[..., -1:]
        dots = jnp.where(dots < thresh, NEG_INF, dots)
        attn = jax.nn.softmax(dots, axis=-1)
        out = jnp.einsum('bhij,bhjd->bhid', attn, v)
        out = out.transpose(0, 2, 1, 3).reshape(b, n, H * DH)
        return out @ Wo + bo

    def _L1_ffn_ref(hidden_states, ln_w, ln_b, router_w, gate_w, up_w, down_w, sh_gate, sh_up, sh_down):
        import jax, jax.numpy as jnp
        import numpy as np
        H = 128
        I = 256
        E = 8
        B, S = (2, 512)
        EPS = 1e-05
        INIT = 0.02

        def _layernorm(x, w, b):
            mu = jnp.mean(x, axis=-1, keepdims=True)
            var = jnp.mean(jnp.square(x - mu), axis=-1, keepdims=True)
            return (x - mu) * jax.lax.rsqrt(var + EPS) * w + b
        b, s, h = hidden_states.shape
        normed = _layernorm(hidden_states, ln_w, ln_b)
        xf = normed.reshape(-1, h)
        logits = xf @ router_w
        top_idx = jnp.argmax(logits, axis=-1)
        top_score = jax.nn.sigmoid(jnp.max(logits, axis=-1))

        def body(acc, ew):
            g, u, d, e = ew
            w = jnp.where(top_idx == e, top_score, 0.0)[:, None]
            xe = xf * w
            hmid = jax.nn.silu(xe @ g) * (xe @ u)
            return (acc + hmid @ d, None)
        routed, _ = jax.lax.scan(body, jnp.zeros_like(xf), (gate_w, up_w, down_w, jnp.arange(E)))
        shared = jax.nn.silu(xf @ sh_gate) * (xf @ sh_up) @ sh_down
        moe_out = (routed + shared).reshape(b, s, h)
        return hidden_states + moe_out
    x = L0_attn_x
    x = x + _layernorm(_L0_attn_ref(_layernorm(x, axis=-1), L0_attn_W_qkv, L0_attn_b_qkv, L0_attn_W_proj, L0_attn_b_proj), axis=-1)
    x = x + _layernorm(_L0_ffn_ref(_layernorm(x, axis=-1), L0_ffn_wi, L0_ffn_bi, L0_ffn_wo, L0_ffn_bo, L0_ffn_lora_A, L0_ffn_lora_B, L0_ffn_gate_w, L0_ffn_gate_b), axis=-1)
    x = x + _layernorm(_L1_attn_ref(_layernorm(x, axis=-1), L1_attn_Wq, L1_attn_Wkv, L1_attn_Wo, L1_attn_bo, L1_attn_pre_proj, L1_attn_post_proj, L1_attn_mem_k, L1_attn_mem_v), axis=-1)
    x = x + _layernorm(_L1_ffn_ref(_layernorm(x, axis=-1), L1_ffn_ln_w, L1_ffn_ln_b, L1_ffn_router_w, L1_ffn_gate_w, L1_ffn_up_w, L1_ffn_down_w, L1_ffn_sh_gate, L1_ffn_sh_up, L1_ffn_sh_down), axis=-1)
    return x

_drawn_inputs = setup_inputs


def setup_inputs(seed=0):
    import zlib

    import numpy as np

    out = dict(_drawn_inputs(seed))
    spreads = {'L0_attn_b_qkv': (0.0, 0.1),
     'L0_attn_b_proj': (0.0, 0.1),
     'L1_attn_bo': (0.0, 0.1),
     'L1_ffn_ln_w': (1.0, 0.6),
     'L1_ffn_ln_b': (0.0, 0.8)}
    factors = {'L0_ffn_bi': 7.699,
     'L0_ffn_bo': 5.639,
     'L0_ffn_gate_b': 26.596,
     'L1_ffn_router_w': 8.0,
     'L1_ffn_gate_w': 8.0,
     'L1_ffn_up_w': 8.0,
     'L1_ffn_down_w': 8.0,
     'L1_ffn_sh_gate': 8.0,
     'L1_ffn_sh_up': 8.0,
     'L1_ffn_sh_down': 8.0}
    for name, (base, spread) in spreads.items():
        noise = np.random.default_rng([zlib.crc32(name.encode()), seed]).standard_normal(out[name].shape)
        drawn = base * np.exp(spread * noise) if base else spread * noise
        out[name] = jnp.asarray(drawn.astype(out[name].dtype))
    for name, factor in factors.items():
        out[name] = (out[name] * factor).astype(out[name].dtype)
    return out
```

```python
from contextlib import ExitStack

import concourse.bass as bass
from concourse import mybir

ALU = mybir.AluOpType
ACT = mybir.ActivationFunctionType
AX = mybir.AxisListType
F32 = mybir.dt.float32

P = 128
TOK = 2048
NT = TOK // P
E0 = 8
FF = 512
H1, DH, MEM, TOPK = 16, 64, 16, 64
INNER = H1 * DH
UNITS = NT * H1
WIDE = MEM + TOK
FI = 256
EPS = 1e-5
LOW = 2.0 ** -30
NS, NA = 4, 3
SC = 1024
DIRECT = set(range(NT))

_INS = ['L0_attn_x', 'L0_attn_W_qkv', 'L0_attn_b_qkv', 'L0_ffn_wi', 'L0_ffn_bi', 'L0_ffn_wo', 'L0_ffn_bo',
        'L0_ffn_lora_A', 'L0_ffn_lora_B', 'L0_ffn_gate_w', 'L0_ffn_gate_b', 'L1_attn_Wq', 'L1_attn_Wkv', 'L1_attn_Wo',
        'L1_attn_bo', 'L1_attn_pre_proj', 'L1_attn_mem_k', 'L1_attn_mem_v', 'L1_ffn_ln_w', 'L1_ffn_ln_b',
        'L1_ffn_router_w', 'L1_ffn_gate_w', 'L1_ffn_up_w', 'L1_ffn_down_w', 'L1_ffn_sh_gate', 'L1_ffn_sh_up',
        'L1_ffn_sh_down']


def wide(t):
    return MEM + P * (t + 1)


def slots(t):
    return -(-wide(t) // SC)


class Fills:

    def __init__(self):
        self.names, self.engine = [], []

    def add(self, name, engine):
        self.names.append(name)
        self.engine.append(engine)

    def index(self, name):
        return self.names.index(name)

    def drained(self, n):
        return self.engine[:n + 1].count(self.engine[n])


def plan_fills():
    f = Fills()
    for b in range(4):
        f.add(("h", 0, b), "act")
    for b in range(8):
        f.add(("kv", b), "act")
    for b in range(4):
        f.add(("q", b), "dve")
    f.add("kvsum", "dve")
    for b in range(8):
        f.add(("att", b), "dve")
    for n in ("wi", "wo", "loraB", "loraA_gate"):
        f.add(n, "act")
    for b in range(4):
        f.add(("h", 1, b), "act")
    f.add("logit0", "dve")
    for b in range(4):
        f.add(("lowrank", b), "dve")
    for k in range(2):
        for b in range(4):
            f.add(("pick", k, b), "act")
    for b in range(4):
        for n in range(8):
            f.add(("mid", b, n), "act")
        f.add(("ffn0", b), "dve")
    for b in range(4):
        f.add(("wqk", b), "act")
    f.add("memk", "act")
    f.add("memscore", "act")
    for g in range(4):
        f.add(("G", g), "act")
    for b in range(4):
        f.add(("h", 2, b), "act")
    for t in range(NT):
        for b in range(2):
            f.add(("v", t, b), "act")
    return f


def plan_ffn1():
    f = Fills()
    for b in range(4):
        f.add(("xf", b), "act")
    f.add("logit1", "dve")
    for b in range(4):
        f.add(("xs", b), "act")

    def up(n):
        for i in range(2):
            f.add(("g", *divmod(n, 4), i), "act")
            f.add(("u", *divmod(n, 4), i), "dve")

    up(0)
    for n in range(4 * (E0 + 1)):
        if n + 1 < 4 * (E0 + 1):
            up(n + 1)
        f.add(("d", *divmod(n, 4)), "dve")
    return f


def build(nc, out, x, Wqkv, bqkv, wi, bi, wo, bo0, loraA, loraB, gate_w, gate_b, Wq, Wkv, Wo, bo1, pre, mem_k, mem_v,
          ln_w, ln_b, router_w, gw1, uw1, dw1, shg, shu, shd):
    fills, ffills = plan_fills(), plan_ffn1()
    with ExitStack() as ctx:
        def sb(name, shape, dt=F32):
            return ctx.enter_context(nc.sbuf_tensor(name, shape, dt))

        def sem(name):
            return ctx.enter_context(nc.semaphore(name))

        X = sb("X", [P, NT, P])
        Y = sb("Y", [P, NT, P])
        hT = sb("hT", [P, TOK])
        BIG = sb("BIG", [P, NT * INNER])
        SA = sb("SA", [P, (NS + NA) * WIDE])
        G = sb("G", [P, H1, P])
        Mk = sb("Mk", [P, H1 * MEM])
        qT = sb("qT", [P, H1, P])
        PT = sb("PT", [P, 4, 512])
        Wo_sb = sb("Wo_sb", [P, 8, P])
        mvd = sb("mvd", [P, 2, 512])
        Pm = sb("Pm", [P, H1, MEM])
        PmT = sb("PmT", [P, 2, P])
        O = sb("O", [P, INNER])
        OT = sb("OT", [P, 8, P])
        m8 = sb("m8", [P, 2, 8, 8])
        negm = sb("negm", [P, 4])
        den = sb("den", [P, 2, H1])
        rden = sb("rden", [P, 2, H1])
        ident = sb("ident", [P, P])
        cmask = sb("cmask", [P, P])
        bdm = sb("bdm", [P, P])
        onerow = sb("onerow", [1, P])
        tworow = sb("tworow", [1, P])
        rank8 = sb("rank8", [P, NT, E0])
        rows = sb("rows", [1, 256 + E0 + P + P])
        bcol = sb("bcol", [P, 1 + 4])
        st6 = sb("st6", [P, NT, 6])
        mv = sb("mv", [P, NT, 2])
        std = sb("std", [P, NT])
        rstd = sb("rstd", [P, NT])
        sm = sb("sm", [P, 8, NT])
        rt = sb("rt", [P, 6, NT, E0])
        lnw = sb("lnw", [P, 2, P])
        rw_sb = sb("rw_sb", [P, E0])
        gwT = sb("gwT", [P, E0])
        w0 = BIG[:, 12288:16384]
        Wqkv_sb = w0[:, 0:384]
        wiT = w0[:, 384:896]
        woT = w0[:, 896:1408].rearrange("p (f d) -> p f d", f=4)
        lAT = w0[:, 1408:1536]
        lBT = w0[:, 1536:2048]
        kvm = w0[:, 2048:2192]
        ksum = w0[:, 2192:2193]
        kvr = BIG[:, 0:NT * 257].rearrange("p (t c) -> p t c", t=NT)
        pqT = BIG[:, 4112:4112 + TOK]
        pickT = BIG[:, 0:2 * TOK].rearrange("p (k c) -> p k c", k=2)
        mid = BIG[:, 4096:4096 + 8192].rearrange("p (r n c) -> p r n c", r=2, n=8)
        V = BIG[:, :].rearrange("p (t c) -> p t c", t=NT)
        T1 = SA[:, 0:2048]
        T2 = SA[:, 2048:4096]
        pick = SA[:, 0:4096].rearrange("p (k t c) -> p k t c", k=2, t=NT)
        wstage = SA[:, 4096:4096 + 1792]
        wi_r = wstage[:, 0:512].rearrange("p (f c) -> p f c", f=4)
        wo_r = wstage[:, 512:1024]
        lB_r = wstage[:, 1024:1536].rearrange("p (f e r) -> p f e r", f=4, e=E0)
        lA_r = wstage[:, 1536:1664]
        gw_r = wstage[0:E0, 1664:1792]
        Wq_r = SA[:, 6144:7168]
        Wk_r = SA[:, 7168:8192]
        mk_r = SA[0:MEM, 8192:9216]
        Wv_sb = SA[:, 9216:10240]
        pre_b = SA[:, 10240:10368].rearrange("p (c k) -> p c k", c=8)
        WqT = SA[:, 4096:5120].rearrange("p (c n) -> p c n", c=8)
        WkT = SA[:, 5120:6144].rearrange("p (c n) -> p c n", c=8)
        mkT = SA[:, 10368:10496].rearrange("p (c m) -> p c m", c=8)
        mkS = SA[:, 2048:4096].rearrange("p (c k m) -> p c k m", c=8, k=H1)
        S = [SA[:, n * WIDE:(n + 1) * WIDE] for n in range(NS)]
        A = [SA[:, (NS + n) * WIDE:(NS + n + 1) * WIDE] for n in range(NA)]
        gw_sb = SA[:, 0:2304].rearrange("p (e i) -> p e i", e=E0 + 1)
        uw_sb = SA[:, 2304:4608].rearrange("p (e i) -> p e i", e=E0 + 1)
        dw_sb = SA[:, 4608:6912].rearrange("p (e i d) -> p e i d", e=E0 + 1, i=2)
        N1 = SA[:, 6912:8960].rearrange("p (t c) -> p t c", t=NT)
        acc = SA[:, 8960:11008].rearrange("p (t c) -> p t c", t=NT)
        xsT = SA[:, 11008:13056]
        sg = BIG[:, 0:2048].rearrange("p (r c) -> p r c", r=4)
        hm = BIG[:, 2048:6144].rearrange("p (r i c) -> p r i c", r=4, i=2)
        XS = BIG[:, 6144:8192].rearrange("p (t c) -> p t c", t=NT)
        WkS = BIG[:, 4096:4096 + 8192].rearrange("p (r c k n) -> p r c k n", r=2, c=8, k=4)

        banks = [ctx.enter_context(nc.psum_tensor(f"bank{n}", [P, 2, 512] if n < 4 and n % 2 == 0 else [P, 512], F32))
                 for n in (0, 2, 4, 5, 6, 7)]
        bank = [banks[0][:, 0, :], banks[0][:, 1, :], banks[1][:, 0, :], banks[1][:, 1, :],
                banks[2][:, :], banks[3][:, :], banks[4][:, :], banks[5][:, :]]
        score = [banks[0][:, :, :].rearrange("p a b -> p (a b)"), banks[1][:, :, :].rearrange("p a b -> p (a b)")]

        s_x, s_w0, s_stage, s_wa, s_mv, s_wf, s_ln = (sem(n) for n in
                                                      ("s_x", "s_w0", "s_stage", "s_wa", "s_mv", "s_wf", "s_ln"))
        s_const = sem("s_const")
        s_dve = sem("s_dve")
        s_act = sem("s_act")
        s_pool = sem("s_pool")
        s_fill = sem("s_fill")
        s_drain_a = sem("s_drain_a")
        s_drain_v = sem("s_drain_v")
        s_rows = sem("s_rows")
        s_var = sem("s_var")
        s_std = sem("s_std")
        s_phi_in, s_phi = sem("s_phi_in"), sem("s_phi")
        s_pk, s_pq = sem("s_pk"), sem("s_pq")
        s_kvm = sem("s_kvm")
        s_logit, s_exp = sem("s_logit"), sem("s_exp")
        s_pick = sem("s_pick")
        s_pre, s_WkS, s_mkS, s_G = sem("s_pre"), sem("s_WkS"), sem("s_mkS"), sem("s_G")
        s_out = sem("s_out")
        s_qfill, s_qT = sem("s_qfill"), sem("s_qT")
        s_sfill, s_sdrain = sem("s_sfill"), sem("s_sdrain")
        s_keep = sem("s_keep")
        s_min = sem("s_min")
        s_prob = sem("s_prob")
        s_pm = sem("s_pm")
        s_tfill, s_tdrain = sem("s_tfill"), sem("s_tdrain")
        s_pv = sem("s_pv")
        s_scr = sem("s_scr")
        s_half = sem("s_half")
        s_pmT = sem("s_pmT")
        s_O = sem("s_O")
        s_y1 = sem("s_y1")
        s_sig_in, s_sig = sem("s_sig_in"), sem("s_sig")
        s_ffill, s_fdrain_a, s_fdrain_v = (sem(n) for n in ("s_ffill", "s_fdrain_a", "s_fdrain_v"))

        sbase = [0] * (UNITS + 1)
        for u in range(UNITS):
            sbase[u + 1] = sbase[u] + slots(u // H1)
        pieces, tbase = [], {}
        for u in range(UNITS):
            t = u // H1
            tbase[u] = len(pieces)
            pieces += [("p", u, n) for n in range(-(-(t + 1) // 4))]
            if u % 8 == 7:
                tbase["m", u // 8] = len(pieces)
                pieces.append(("m", u // 8, 0))
            for v in ([t - 1] if u % H1 == 3 and t else []) + ([t] if u == UNITS - 1 else []):
                tbase["o", v] = len(pieces)
                pieces += [("o", v, 0), ("o", v, 1), ("y", v, 0)]
        pcount, count = {}, 0
        for n, piece in enumerate(pieces):
            pcount[n] = count
            count += piece[0] == "p"

        block = ctx.enter_context(nc.Block())

        @block.sync
        def _(sp):
            sp.dma_start(X[:, :, :], x[0].rearrange("(t p) c -> p t c", p=P)).then_inc(s_x, 16)
            sp.dma_start(Wqkv_sb, Wqkv).then_inc(s_w0, 16)
            sp.dma_start(wi_r, wi.rearrange("(f p) c -> p f c", p=P)).then_inc(s_stage, 16)
            sp.dma_start(wo_r, wo).then_inc(s_stage, 16)
            for f in range(4):
                sp.dma_start(lB_r[:, f], loraB[:, f * P:(f + 1) * P, :].rearrange("e f r -> f e r")).then_inc(s_stage, 16)
            sp.dma_start(lA_r, loraA.rearrange("e r c -> (e r) c")).then_inc(s_stage, 16)
            sp.dma_start(gw_r, gate_w).then_inc(s_stage, 16)
            sp.wait_ge(s_tfill, len(pieces))
            sp.wait_ge(s_pm, UNITS)
            sp.dma_start(gw_sb[:, 0:E0, :], gw1.rearrange("e c i -> c e i")).then_inc(s_wf, 16)
            sp.dma_start(uw_sb[:, 0:E0, :], uw1.rearrange("e c i -> c e i")).then_inc(s_wf, 16)
            sp.dma_start(dw_sb[:, 0:E0], dw1.rearrange("e (i p) d -> p e i d", p=P)).then_inc(s_wf, 16)
            sp.dma_start(gw_sb[:, E0, :], shg).then_inc(s_wf, 16)
            sp.dma_start(uw_sb[:, E0, :], shu).then_inc(s_wf, 16)
            sp.dma_start(dw_sb[:, E0], shd.rearrange("(i p) d -> p i d", p=P)).then_inc(s_wf, 16)
            sp.wait_ge(s_y1, 1)
            sp.dma_start(out[0].rearrange("(t p) c -> p t c", p=P), X[:, :, :]).then_inc(s_out, 16)
            sp.wait_ge(s_out, 16)

        @block.gpsimd
        def _(pool):
            pool.memset(ident[:, :], 0.0).then_inc(s_pool, 1)
            pool.memset(cmask[:, :], 0.0).then_inc(s_pool, 1)
            pool.memset(bdm[:, :], 1.0).then_inc(s_pool, 1)
            pool.memset(onerow[:, :], 1.0).then_inc(s_const, 1)
            pool.memset(tworow[:, :], 2.0).then_inc(s_const, 1)
            pool.memset(kvr[:, :, 256:257], 1.0).then_inc(s_const, 1)
            pool.memset(mvd[:, :, :], 0.0).then_inc(s_pool, 1)
            for n in range(E0):
                pool.memset(rank8[:, :, n:n + 1], float(E0 - n)).then_inc(s_const, 1)
            pool.wait_ge(s_pool, 4)
            pool.affine_select(out=ident[:, :], in_=ident[:, :], compare_op=ALU.not_equal, fill=1.0, base=0,
                               pattern=[[-1, P]], channel_multiplier=1).then_inc(s_const, 1)
            pool.affine_select(out=cmask[:, :], in_=cmask[:, :], compare_op=ALU.is_ge, fill=-1.0, base=0,
                               pattern=[[-1, P]], channel_multiplier=1).then_inc(s_const, 1)
            b3 = bdm[:, :].rearrange("p (b m) -> p b m", b=16)
            pool.affine_select(out=b3, in_=b3, compare_op=ALU.is_ge, fill=0.0, base=0,
                               pattern=[[-8, 16], [0, 8]], channel_multiplier=1).then_inc(s_pool, 1)
            pool.wait_ge(s_pool, 5)
            pool.affine_select(out=b3, in_=b3, compare_op=ALU.is_ge, fill=0.0, base=7,
                               pattern=[[8, 16], [0, 8]], channel_multiplier=-1).then_inc(s_const, 1)
            for h in range(H1):
                pool.dma_start(mvd[MEM * (h % 8):MEM * (h % 8 + 1), h // 8, DH * (h % 8):DH * (h % 8 + 1)],
                               mem_v[h]).then_inc(s_mv, 16)
            for s in range(UNITS + 4):
                if 2 <= s < UNITS + 2:
                    u = s - 2
                    n = wide(u // H1)
                    pool.wait_ge(s_keep, u + 1)
                    pool.tensor_tensor(A[u % NA][:, 0:n], S[u % NS][:, 0:n], A[u % NA][:, 0:n], ALU.add)\
                        .then_inc(s_min, 1)
                if 3 <= s < UNITS + 3:
                    u = s - 3
                    pool.wait_ge(s_prob, u + 1)
                    if u % 8 == 0 and u >= 16:
                        pool.wait_ge(s_tfill, tbase["m", u // 8 - 2] + 1)
                    pool.tensor_copy(Pm[:, u % H1, :], A[u % NA][:, 0:MEM]).then_inc(s_pm, 1)

        @block.scalar
        def _(act):
            acts = [0]

            def link(ins):
                acts[0] += 1
                ins.then_inc(s_act, 1)
                act.wait_ge(s_act, acts[0])

            def drain(name, dst, func=ACT.Copy, src=lambda b: b, **kw):
                n = fills.index(name)
                act.wait_ge(s_fill, n + 1)
                act.activation(dst, src(bank[n % 8]), func, **kw).then_inc(s_drain_a, 1)

            def sqrt(n):
                act.wait_ge(s_var, n)
                act.activation(std[:, :], mv[:, :, 1], ACT.Sqrt).then_inc(s_std, 1)

            act.dma_start(bcol[:, 0:1], bqkv[0:P].rearrange("(p a) -> p a", a=1)).then_inc(s_w0, 16)
            act.dma_start(rows[:, 0:256], bqkv[P:3 * P].rearrange("(a n) -> a n", a=1)).then_inc(s_w0, 16)
            act.dma_start(rows[:, 256:264], gate_b.rearrange("(a n) -> a n", a=1)).then_inc(s_w0, 16)
            act.dma_start(rows[:, 264:392], bo0.rearrange("(a n) -> a n", a=1)).then_inc(s_w0, 16)
            act.dma_start(rows[:, 392:520], bo1.rearrange("(a n) -> a n", a=1)).then_inc(s_w0, 16)
            with nc.allow_non_contiguous_dma(reason="bias by feature"):
                act.dma_start(bcol[:, 1:5], bi.rearrange("(f p) -> p f", p=P)).then_inc(s_w0, 16)
            act.dma_start(lnw[:, 0, :], ln_w.rearrange("(a n) -> a n", a=1).to_broadcast([P, P])).then_inc(s_ln, 16)
            act.dma_start(lnw[:, 1, :], ln_b.rearrange("(a n) -> a n", a=1).to_broadcast([P, P])).then_inc(s_ln, 16)
            act.dma_start(rw_sb[:, :], router_w).then_inc(s_ln, 16)
            act.dma_start(Wq_r, Wq).then_inc(s_wa, 16)
            act.dma_start(Wk_r, Wkv[:, 0:INNER]).then_inc(s_wa, 16)
            act.dma_start(Wv_sb, Wkv[:, INNER:2 * INNER]).then_inc(s_wa, 16)
            act.dma_start(mk_r.rearrange("m (h d) -> m h d", h=H1), mem_k.rearrange("h m d -> m h d")).then_inc(s_wa, 16)
            act.dma_start(Wo_sb[:, :, :], Wo.rearrange("(c p) n -> p c n", p=P)).then_inc(s_wa, 16)
            for j in range(2):
                act.dma_start(pre_b[DH * j:DH * (j + 1)],
                              pre.rearrange("(c j) k -> j c k", j=2)[j:j + 1].to_broadcast([DH, 8, H1])).then_inc(s_wa, 16)

            sqrt(1)
            for b in range(4):
                drain(("h", 0, b), hT[:, 512 * b:512 * b + 512])
            for b in range(8):
                drain(("kv", b), kvr[:, 2 * b:2 * b + 2, 0:256], src=lambda k: k.rearrange("p (t c) -> p t c", t=2))
            for n in range(2):
                act.wait_ge(s_phi_in, n + 1)
                act.activation((T1, T2)[n], (T1, T2)[n], ACT.Exp).then_inc(s_phi, 1)
            sqrt(2)
            drain("wi", wiT)
            drain("wo", woT.rearrange("p f d -> p (f d)"))
            drain("loraB", lBT)
            n = fills.index("loraA_gate")
            act.wait_ge(s_fill, n + 1)
            act.activation(lAT, bank[n % 8][:, 0:P], ACT.Copy)
            act.activation(gwT[:, :], bank[n % 8][:, P:P + E0], ACT.Copy).then_inc(s_drain_a, 1)
            sqrt(3)
            for b in range(4):
                drain(("h", 1, b), hT[:, 512 * b:512 * b + 512])
            act.wait_ge(s_logit, 1)
            act.activation(rt[:, 0], rt[:, 0], ACT.Exp).then_inc(s_exp, 1)
            for k in range(2):
                for b in range(4):
                    drain(("pick", k, b), pickT[:, k, 512 * b:512 * b + 512])
            for b in range(4):
                for n in range(8):
                    if n == 0 and b >= 2:
                        act.wait_ge(s_fill, fills.index(("ffn0", b - 2)) + 1)
                    drain(("mid", b, n), mid[:, b % 2, n, :], ACT.Relu, bias=bcol[:, 1 + n % 4:2 + n % 4])
            for b in range(4):
                drain(("wqk", b), (WqT if b < 2 else WkT)[:, 4 * (b % 2):4 * (b % 2) + 4, :].rearrange("p c n -> p (c n)"))
            drain("memk", mkT.rearrange("p c m -> p (c m)"), src=lambda k: k[:, 0:P])
            drain("memscore", Mk[:, :], src=lambda k: k[:, 0:H1 * MEM])
            for g in range(4):
                drain(("G", g), G[:, 4 * g:4 * g + 4, :].rearrange("p k n -> p (k n)"))
            sqrt(4)
            sqrt(5)
            for b in range(4):
                drain(("h", 2, b), hT[:, 512 * b:512 * b + 512])
            for t in range(NT):
                for b in range(2):
                    drain(("v", t, b), V[:, t, 512 * b:512 * b + 512])

            def scores(u):
                t = u // H1
                if u % H1 == 0:
                    for h in range(2):
                        act.wait_ge(s_qfill, 2 * t + h + 1)
                        act.activation(qT[:, 8 * h:8 * h + 8, :].rearrange("p k n -> p (k n)"), score[h], ACT.Copy)\
                            .then_inc(s_qT, 1)
                if u >= NS:
                    act.wait_ge(s_min, u - NS + 1)
                for c in range(slots(t)):
                    w = min(SC, wide(t) - SC * c)
                    act.wait_ge(s_sfill, sbase[u] + c + 1)
                    act.activation(S[u % NS][:, SC * c:SC * c + w], score[(sbase[u] + c) % 2][:, 0:w], ACT.Copy)\
                        .then_inc(s_sdrain, 1)

            def turned(first, count):
                for n in range(first, first + count):
                    kind, v, c = pieces[n]
                    act.wait_ge(s_tfill, n + 1)
                    src = bank[4 + n % 2]
                    if kind == "p":
                        w = min(512, P * (v // H1 + 1) - 512 * c)
                        k = pcount[n]
                        if k >= 4:
                            act.wait_ge(s_pv, k - 3)
                        act.activation(PT[:, k % 4, 0:w], src[:, 0:w], ACT.Copy).then_inc(s_tdrain, 1)
                    elif kind == "m":
                        act.activation(PmT[:, v % 2, :], src[:, 0:P], ACT.Copy).then_inc(s_tdrain, 1)
                    elif kind == "o":
                        act.activation(OT[:, 4 * c:4 * c + 4, :].rearrange("p c n -> p (c n)"), src, ACT.Copy)\
                            .then_inc(s_tdrain, 1)
                    else:
                        act.activation(Y[:, v, :], src[:, 0:P], ACT.Copy).then_inc(s_tdrain, 1)

            for s in range(-1, UNITS + 3):
                if s + 1 < UNITS:
                    scores(s + 1)
                u = s - 3
                if 0 <= u < UNITS:
                    n = wide(u // H1)
                    act.wait_ge(s_min, u + 1)
                    act.activation(A[u % NA][:, 0:n], A[u % NA][:, 0:n], ACT.Exp, bias=negm[:, u % 4:u % 4 + 1],
                                   scale=1.0 / LOW, accum_out=den[:, u // H1 % 2, u % H1:u % H1 + 1]).then_inc(s_prob, 1)
                    end = tbase[u + 1] if u + 1 < UNITS else len(pieces)
                    turned(tbase[u], end - tbase[u])

            def fdrain(name, dst, func=ACT.Copy, **kw):
                n = ffills.index(name)
                act.wait_ge(s_ffill, n + 1)
                act.activation(dst, bank[n % 8], func, **kw).then_inc(s_fdrain_a, 1)

            sqrt(6)
            sqrt(7)
            sqrt(8)
            for b in range(4):
                fdrain(("xf", b), hT[:, 512 * b:512 * b + 512])
            act.wait_ge(s_sig_in, 1)
            act.activation(sm[:, 5, :], sm[:, 4, :], ACT.Sigmoid).then_inc(s_sig, 1)
            for b in range(4):
                fdrain(("xs", b), xsT[:, 512 * b:512 * b + 512])
            for e in range(E0 + 1):
                for b in range(4):
                    for i in range(2):
                        k = (e * 4 + b) * 2 + i
                        if k >= 4:
                            m = (k - 4) // 2
                            act.wait_ge(s_fdrain_v, ffills.drained(ffills.index(("u", *divmod(m, 4), k % 2))))
                        fdrain(("g", e, b, i), sg[:, k % 4, :], ACT.Silu)
            sqrt(9)

        @block.tensor
        def _(pe):
            def open_fill(name):
                n = fills.index(name)
                if n >= 8:
                    m = n - 8
                    pe.wait_ge(s_drain_a if fills.engine[m] == "act" else s_drain_v, fills.drained(m))
                return bank[n % 8]

            def turn_rows(which, count, src):
                pe.wait_ge(s_rows, count)
                for b in range(4):
                    k = open_fill((which[0], which[1], b))
                    for i in range(4):
                        last = pe.transpose(k[:, P * i:P * i + P], src[:, 4 * b + i, :], ident[:, :])
                    last.then_inc(s_fill, 1)

            pe.wait_ge(s_const, 3 + E0 + 3)
            turn_rows(("h", 0), 1, Y)
            pe.wait_ge(s_w0, 16 * 7)
            pe.wait_ge(s_drain_a, 4)
            for b in range(8):
                k = open_fill(("kv", b))
                for i in range(2):
                    t = 2 * b + i
                    pe.matmul(k[:, 256 * i:256 * i + 256], hT[:, P * t:P * t + P], Wqkv_sb[:, P:3 * P], start=True, stop=False)
                    last = pe.matmul(k[:, 256 * i:256 * i + 256], onerow[:, :], rows[:, 0:256], start=False, stop=True)
                last.then_inc(s_fill, 1)
            for b in range(4):
                k = open_fill(("q", b))
                pe.matmul(k, Wqkv_sb[:, 0:P], hT[:, 512 * b:512 * b + 512], start=True, stop=True).then_inc(s_fill, 1)
            pe.wait_ge(s_pk, 1)
            k = open_fill("kvsum")
            for t in range(NT):
                last = pe.matmul(k[:, 0:P + 1], kvr[:, t, 0:P], kvr[:, t, P:257], start=(t == 0), stop=(t == NT - 1))
            last.then_inc(s_fill, 1)
            pe.wait_ge(s_pq, 1)
            pe.wait_ge(s_kvm, 1)
            for b in range(8):
                k = open_fill(("att", b))
                for i in range(2):
                    t = 2 * b + i
                    last = pe.matmul(k[:, 256 * i:256 * i + 144], pqT[:, P * t:P * t + P], kvm, start=True, stop=True)
                last.then_inc(s_fill, 1)
            pe.wait_ge(s_stage, 16 * 8)
            k = open_fill("wi")
            for f in range(4):
                last = pe.transpose(k[:, P * f:P * f + P], wi_r[:, f, :], ident[:, :])
            last.then_inc(s_fill, 1)
            k = open_fill("wo")
            for f in range(4):
                last = pe.transpose(k[:, P * f:P * f + P], wo_r[:, P * f:P * f + P], ident[:, :])
            last.then_inc(s_fill, 1)
            k = open_fill("loraB")
            for f in range(4):
                last = pe.transpose(k[:, P * f:P * f + P], lB_r[:, f].rearrange("p e r -> p (e r)"), ident[:, :])
            last.then_inc(s_fill, 1)
            k = open_fill("loraA_gate")
            pe.transpose(k[:, 0:P], lA_r, ident[:, :])
            pe.transpose(k[:, P:P + E0], gw_r, ident[0:E0, 0:E0]).then_inc(s_fill, 1)
            turn_rows(("h", 1), 2, Y)
            pe.wait_ge(s_drain_a, fills.drained(fills.index(("h", 1, 3))))
            k = open_fill("logit0")
            for t in range(NT):
                pe.matmul(k[:, E0 * t:E0 * t + E0], hT[:, P * t:P * t + P], gwT[:, :], start=True, stop=False)
                last = pe.matmul(k[:, E0 * t:E0 * t + E0], onerow[:, :], rows[:, 256:264], start=False, stop=True)
            last.then_inc(s_fill, 1)
            for b in range(4):
                k = open_fill(("lowrank", b))
                for i in range(4):
                    t = 4 * b + i
                    last = pe.matmul(k[:, P * i:P * i + P], hT[:, P * t:P * t + P], lAT, start=True, stop=True)
                last.then_inc(s_fill, 1)
            for n in range(2):
                pe.wait_ge(s_pick, n + 1)
                for b in range(4):
                    k = open_fill(("pick", n, b))
                    for i in range(4):
                        last = pe.transpose(k[:, P * i:P * i + P], pick[:, n, 4 * b + i, :], ident[:, :])
                    last.then_inc(s_fill, 1)
            pe.wait_ge(s_drain_a, fills.drained(fills.index(("pick", 1, 3))))

            def mids(b):
                for n in range(8):
                    k = open_fill(("mid", b, n))
                    f = n % 4
                    pe.matmul(k, wiT[:, P * f:P * f + P], hT[:, 512 * b:512 * b + 512], start=True, stop=False)
                    pe.matmul(k, lBT[:, P * f:P * f + P], pickT[:, n // 4, 512 * b:512 * b + 512], start=False, stop=True)\
                        .then_inc(s_fill, 1)

            for b in range(4):
                mids(b)
                pe.wait_ge(s_drain_a, fills.drained(fills.index(("mid", b, 7))))
                k = open_fill(("ffn0", b))
                for i in range(4):
                    o = k[:, P * i:P * i + P]
                    for n in range(8):
                        pe.matmul(o, mid[:, b % 2, n, P * i:P * i + P], woT[:, n % 4, :], start=(n == 0), stop=False)
                    last = pe.matmul(o, tworow[:, :], rows[:, 264:392], start=False, stop=True)
                last.then_inc(s_fill, 1)
            pe.wait_ge(s_wa, 16 * 7)
            for b in range(4):
                k = open_fill(("wqk", b))
                for i in range(4):
                    c = 4 * (b % 2) + i
                    last = pe.transpose(k[:, P * i:P * i + P], (Wq_r if b < 2 else Wk_r)[:, P * c:P * c + P], ident[:, :])
                last.then_inc(s_fill, 1)
            k = open_fill("memk")
            for c in range(8):
                last = pe.transpose(k[:, MEM * c:MEM * c + MEM], mk_r[:, P * c:P * c + P], ident[0:MEM, 0:MEM])
            last.then_inc(s_fill, 1)
            k = open_fill("memscore")
            pe.wait_ge(s_mkS, 1)
            for c in range(8):
                last = pe.matmul(k[:, 0:H1 * MEM], WqT[:, c, :], mkS[:, c].rearrange("p k m -> p (k m)"),
                                 start=(c == 0), stop=(c == 7))
            last.then_inc(s_fill, 1)
            for g in range(4):
                k = open_fill(("G", g))
                pe.wait_ge(s_WkS, g + 1)
                for c in range(8):
                    last = pe.matmul(k, WqT[:, c, :], WkS[:, g % 2, c].rearrange("p k n -> p (k n)"),
                                     start=(c == 0), stop=(c == 7))
                last.then_inc(s_fill, 1)
            turn_rows(("h", 2), 3, Y)
            pe.wait_ge(s_drain_a, fills.drained(fills.index(("h", 2, 3))))
            for t in range(NT):
                for b in range(2):
                    k = open_fill(("v", t, b))
                    pe.matmul(k, hT[:, P * t:P * t + P], Wv_sb[:, 512 * b:512 * b + 512], start=True, stop=True)\
                        .then_inc(s_fill, 1)
            pe.wait_ge(s_drain_a, fills.engine.count("act"))
            pe.wait_ge(s_drain_v, fills.engine.count("dve"))
            pe.wait_ge(s_mv, 16 * H1)

            def scores(u):
                t, h = divmod(u, H1)
                if h == 0:
                    if u:
                        pe.wait_ge(s_sdrain, sbase[u])
                    for g in range(2):
                        for i in range(8):
                            last = pe.matmul(score[g][:, P * i:P * i + P], G[:, 8 * g + i, :], hT[:, P * t:P * t + P],
                                             start=True, stop=True)
                        last.then_inc(s_qfill, 1)
                    pe.wait_ge(s_qT, 2 * t + 2)
                n = wide(t)
                for c in range(-(-n // 512)):
                    slot = sbase[u] + c // 2
                    if c % 2 == 0 and slot - 2 >= sbase[u - h]:
                        pe.wait_ge(s_sdrain, slot - 1)
                    a, b = 512 * c, min(512 * c + 512, n)
                    to = score[slot % 2][:, a - SC * (c // 2):b - SC * (c // 2)]
                    d0 = max(a, n - P)
                    masked = d0 < b
                    if c == 0:
                        pe.matmul(to[:, 0:MEM], hT[:, P * t:P * t + P], Mk[:, MEM * h:MEM * h + MEM], start=True, stop=False,
                                  skip_group_check=True)
                        last = pe.matmul(to[:, MEM:], qT[:, h, :], hT[:, 0:b - MEM], start=False, stop=not masked,
                                         skip_group_check=True)
                    else:
                        last = pe.matmul(to, qT[:, h, :], hT[:, a - MEM:b - MEM], start=True, stop=not masked,
                                         skip_group_check=True)
                    if masked:
                        last = pe.matmul(to[:, d0 - a:b - a], ident[:, :], cmask[:, d0 - (n - P):b - (n - P)], start=False,
                                         stop=True, skip_group_check=True)
                    if c % 2 or b == n:
                        last.then_inc(s_sfill, 1)

            def values(u):
                t, h = divmod(u, H1)
                pe.wait_ge(s_prob, u + 1)
                acc_bank = bank[6 + h // 8]
                if h % 8 == 0 and t:
                    pe.wait_ge(s_O, 2 * t - 1 + h // 8)
                n0 = tbase[u]
                np_ = -(-(t + 1) // 4)

                def turn(c):
                    n = n0 + c
                    if n >= 2:
                        pe.wait_ge(s_tdrain, n - 1)
                    blocks = min(4, t + 1 - 4 * c)
                    for i in range(blocks):
                        j = 4 * c + i
                        last = pe.transpose(bank[4 + n % 2][:, P * i:P * i + P],
                                            A[u % NA][:, MEM + P * j:MEM + P * j + P], ident[:, :])
                    last.then_inc(s_tfill, 1)

                def product(c):
                    n = n0 + c
                    pe.wait_ge(s_tdrain, n + 1)
                    blocks = min(4, t + 1 - 4 * c)
                    for i in range(blocks):
                        j = 4 * c + i
                        last = pe.matmul(acc_bank[:, DH * (h % 8):DH * (h % 8) + DH], PT[:, pcount[n] % 4, P * i:P * i + P],
                                         V[:, j, DH * h:DH * h + DH], start=(j == 0 and h % 8 == 0), stop=False,
                                         skip_group_check=True)
                    last.then_inc(s_pv, 1)

                turn(0)
                for c in range(np_):
                    if c + 1 < np_:
                        turn(c + 1)
                    product(c)
                if h % 8 == 7:
                    g = h // 8
                    n = tbase["m", u // 8]
                    pe.wait_ge(s_tdrain, n - 1)
                    pe.wait_ge(s_pm, u + 1)
                    pe.transpose(bank[4 + n % 2][:, 0:P], Pm[:, 8 * g:8 * g + 8, :].rearrange("p h m -> p (h m)"),
                                 ident[:, :]).then_inc(s_tfill, 1)
                    pe.wait_ge(s_tdrain, n + 1)
                    pe.matmul(acc_bank, PmT[:, g, :], mvd[:, g, :], start=False, stop=True, skip_group_check=True)\
                        .then_inc(s_half, 1)
                for v in ([t - 1] if h == 3 and t else []) + ([t] if u == UNITS - 1 else []):
                    n = tbase["o", v]
                    pe.wait_ge(s_O, 2 * v + 2)
                    for g in range(2):
                        pe.wait_ge(s_tdrain, n + g - 1)
                        for i in range(4):
                            last = pe.transpose(bank[4 + (n + g) % 2][:, P * i:P * i + P],
                                                O[:, P * (4 * g + i):P * (4 * g + i) + P], ident[:, :])
                        last.then_inc(s_tfill, 1)
                    pe.wait_ge(s_tdrain, n + 2)
                    y = bank[4 + (n + 2) % 2][:, 0:P]
                    for i in range(8):
                        pe.matmul(y, OT[:, i, :], Wo_sb[:, i, :], start=(i == 0), stop=False)
                    pe.matmul(y, onerow[:, :], rows[:, 392:520], start=False, stop=True).then_inc(s_tfill, 1)

            for s in range(-1, UNITS + 3):
                if s + 1 < UNITS:
                    scores(s + 1)
                if 0 <= s - 3 < UNITS:
                    values(s - 3)

            def open_ffill(name):
                n = ffills.index(name)
                if n >= 8:
                    m = n - 8
                    pe.wait_ge(s_fdrain_a if ffills.engine[m] == "act" else s_fdrain_v, ffills.drained(m))
                return bank[n % 8]

            pe.wait_ge(s_tdrain, len(pieces))
            pe.wait_ge(s_rows, 4)
            for b in range(4):
                k = open_ffill(("xf", b))
                for i in range(4):
                    last = pe.transpose(k[:, P * i:P * i + P], N1[:, 4 * b + i, :], ident[:, :])
                last.then_inc(s_ffill, 1)
            pe.wait_ge(s_fdrain_a, 4)
            pe.wait_ge(s_ln, 48)
            k = open_ffill("logit1")
            for t in range(NT):
                last = pe.matmul(k[:, E0 * t:E0 * t + E0], hT[:, P * t:P * t + P], rw_sb[:, :], start=True, stop=True)
            last.then_inc(s_ffill, 1)
            pe.wait_ge(s_rows, 5)
            for b in range(4):
                k = open_ffill(("xs", b))
                for i in range(4):
                    last = pe.transpose(k[:, P * i:P * i + P], XS[:, 4 * b + i, :], ident[:, :])
                last.then_inc(s_ffill, 1)
            pe.wait_ge(s_fdrain_a, 8)
            pe.wait_ge(s_wf, 16 * 6)

            def up(n):
                e, b = divmod(n, 4)
                src = (xsT if e < E0 else hT[:, :])[:, 512 * b:512 * b + 512]
                for i in range(2):
                    for kind, w in (("g", gw_sb), ("u", uw_sb)):
                        k = open_ffill((kind, e, b, i))
                        pe.matmul(k, w[:, e, P * i:P * i + P], src, start=True, stop=True).then_inc(s_ffill, 1)

            def down(n):
                e, b = divmod(n, 4)
                pe.wait_ge(s_fdrain_v, ffills.drained(ffills.index(("u", e, b, 1))))
                k = open_ffill(("d", e, b))
                for i in range(4):
                    for c in range(2):
                        last = pe.matmul(k[:, P * i:P * i + P], hm[:, n % 4, c, P * i:P * i + P], dw_sb[:, e, c, :],
                                         start=(c == 0), stop=(c == 1))
                last.then_inc(s_ffill, 1)

            up(0)
            for n in range(4 * (E0 + 1)):
                if n + 1 < 4 * (E0 + 1):
                    up(n + 1)
                down(n)

        @block.vector
        def _(dve):
            done = [0]

            def mark(ins):
                done[0] += 1
                ins.then_inc(s_dve, 1)

            def link(ins):
                mark(ins)
                dve.wait_ge(s_dve, done[0])

            norms = [0]

            def normalize(src, dst):
                norms[0] += 1
                for t in range(NT):
                    mark(dve.bn_stats(st6[:, t, :], src[:, t, :]))
                dve.wait_ge(s_dve, done[0])
                for t in range(NT):
                    mark(dve.bn_aggr(mv[:, t, :], st6[:, t, :]))
                dve.wait_ge(s_dve, done[0])
                dve.tensor_scalar(mv[:, :, 1], mv[:, :, 1], EPS, None, ALU.add).then_inc(s_var, 1)
                dve.wait_ge(s_std, norms[0])
                link(dve.reciprocal(rstd[:, :], std[:, :]))
                for t in range(NT):
                    mark(dve.tensor_scalar(dst[:, t, :], src[:, t, :], mv[:, t, 0:1], rstd[:, t:t + 1],
                                           ALU.subtract, ALU.mult))
                dve.wait_ge(s_dve, done[0])

            def drained(name):
                n = fills.index(name)
                dve.wait_ge(s_fill, n + 1)
                return bank[n % 8]

            def bc(ap, n):
                return ap.unsqueeze(len(ap.shape)).to_broadcast(list(ap.shape) + [n])

            T1r = T1.rearrange("p (t c) -> p t c", t=NT)

            dve.wait_ge(s_x, 16)
            normalize(X, Y)
            dve.sem_inc(s_rows, 1)
            for b in range(4):
                k = drained(("q", b))
                dve.tensor_scalar(pqT[:, 512 * b:512 * b + 512], k, bcol[:, 0:1], None, ALU.add).then_inc(s_drain_v, 1)
            keys = kvr[:, :, 0:P]
            dve.wait_ge(s_drain_a, fills.drained(fills.index(("kv", 7))))
            dve.tensor_scalar(T1r, keys, 0.0, None, ALU.min).then_inc(s_phi_in, 1)
            dve.wait_ge(s_drain_v, 4)
            dve.tensor_scalar(T2, pqT, 0.0, None, ALU.min).then_inc(s_phi_in, 1)
            dve.wait_ge(s_phi, 1)
            dve.scalar_tensor_tensor(out=keys, in0=keys, scalar=0.0, in1=T1r, op0=ALU.max, op1=ALU.add).then_inc(s_pk, 1)
            dve.wait_ge(s_phi, 2)
            dve.scalar_tensor_tensor(out=pqT, in0=pqT, scalar=0.0, in1=T2, op0=ALU.max, op1=ALU.add).then_inc(s_pq, 1)
            k = drained("kvsum")
            dve.wait_ge(s_const, 3 + E0 + 3)
            mark(dve.tensor_tensor(kvm[:, 0:P], k[:, 0:P], bdm[:, :], ALU.mult))
            dve.tensor_copy(ksum, k[:, P:P + 1]).then_inc(s_drain_v, 1)
            dve.wait_ge(s_drain_v, 5)
            dve.wait_ge(s_dve, done[0])
            dve.tensor_scalar(kvm[:, P:P + 16], bdm[:, :].rearrange("p (b m) -> p b m", b=16)[:, :, 0], ksum, None,
                              ALU.mult).then_inc(s_kvm, 1)
            for b in range(8):
                k = drained(("att", b)).rearrange("p (t c) -> p t c", t=2)
                d = sm[:, 0:4, :].rearrange("p a t -> p (a t)")[:, 0:32].rearrange("p (t h) -> p t h", t=2)
                link(dve.tensor_scalar(d, k[:, :, P:P + 16], 1e-6, None, ALU.add))
                link(dve.reciprocal(d, d))
                dve.tensor_tensor(Y[:, 2 * b:2 * b + 2, :].rearrange("p t (h m) -> p t h m", h=16),
                                  k[:, :, 0:P].rearrange("p t (h m) -> p t h m", h=16), bc(d, 8), ALU.mult)\
                    .then_inc(s_drain_v, 1)
                dve.wait_ge(s_drain_v, 6 + b)
            normalize(Y, T1r)
            link(dve.tensor_tensor(X[:, :, :], X[:, :, :], T1r, ALU.add))
            normalize(X, Y)
            dve.sem_inc(s_rows, 1)
            k = drained("logit0")
            L, oh1, oh2, tmp = rt[:, 0], rt[:, 1], rt[:, 2], rt[:, 3]
            dve.tensor_copy(L.rearrange("p t e -> p (t e)"), k[:, 0:NT * E0]).then_inc(s_drain_v, 1)
            dve.wait_ge(s_drain_v, fills.drained(fills.index("logit0")))
            link(dve.tensor_reduce(sm[:, 0, :], L, AX.X, ALU.max))
            dve.tensor_tensor(L, L, bc(sm[:, 0, :], E0), ALU.subtract).then_inc(s_logit, 1)
            dve.wait_ge(s_exp, 1)
            link(dve.tensor_reduce(sm[:, 1, :], L, AX.X, ALU.add))
            dve.wait_ge(s_const, 3 + E0 + 3)

            def first_max(values, best, onehot):
                link(dve.tensor_reduce(best, values, AX.X, ALU.max))
                link(dve.tensor_tensor(tmp, values, bc(best, E0), ALU.is_equal))
                link(dve.tensor_tensor(tmp, tmp, rank8[:, :, :], ALU.mult))
                link(dve.tensor_reduce(sm[:, 7, :], tmp, AX.X, ALU.max))
                link(dve.tensor_tensor(onehot, tmp, bc(sm[:, 7, :], E0), ALU.is_equal))

            first_max(L, sm[:, 2, :], oh1)
            link(dve.scalar_tensor_tensor(out=L, in0=oh1, scalar=-2.0, in1=L, op0=ALU.mult, op1=ALU.add))
            first_max(L, sm[:, 3, :], oh2)
            link(dve.tensor_tensor(sm[:, 2, :], sm[:, 2, :], sm[:, 3, :], ALU.add))
            link(dve.reciprocal(sm[:, 1, :], sm[:, 1, :]))
            link(dve.tensor_tensor(sm[:, 2, :], sm[:, 2, :], sm[:, 1, :], ALU.mult))
            for n in range(2):
                for b in range(4):
                    k = drained(("lowrank", b)).rearrange("p (t e r) -> p t e r", t=4, e=E0)
                    ins = dve.tensor_tensor(pick[:, n, 4 * b:4 * b + 4, :].rearrange("p t (e r) -> p t e r", e=E0), k,
                                            bc((oh1, oh2)[n][:, 4 * b:4 * b + 4, :], MEM), ALU.mult)
                    if n == 1:
                        ins.then_inc(s_drain_v, 1)
                    else:
                        mark(ins)
                dve.wait_ge(s_dve, done[0])
                if n:
                    dve.wait_ge(s_drain_v, fills.drained(fills.index(("lowrank", 3))))
                dve.sem_inc(s_pick, 1)
            for b in range(4):
                k = drained(("ffn0", b))
                for i in range(4):
                    t = 4 * b + i
                    ins = dve.tensor_scalar(Y[:, t, :], k[:, P * i:P * i + P], sm[:, 2, t:t + 1], None, ALU.mult)
                    if i < 3:
                        mark(ins)
                ins.then_inc(s_drain_v, 1)
                if b == 1:
                    dve.wait_ge(s_wa, 16 * 7)
                    link(dve.tensor_scalar(pre_b, pre_b, DH ** -0.5 * LOW, None, ALU.mult))
            dve.wait_ge(s_dve, done[0])
            dve.wait_ge(s_drain_v, fills.drained(fills.index(("ffn0", 3))))
            dve.wait_ge(s_drain_a, fills.drained(fills.index("memk")))
            dve.tensor_tensor(mkS, mkT.unsqueeze(2).to_broadcast([P, 8, H1, MEM]), bc(pre_b, MEM), ALU.mult)\
                .then_inc(s_mkS, 1)
            for g in range(4):
                if g >= 2:
                    dve.wait_ge(s_fill, fills.index(("G", g - 2)) + 1)
                for c in range(8):
                    ins = dve.tensor_tensor(WkS[:, g % 2, c], WkT[:, c, :].unsqueeze(1).to_broadcast([P, 4, P]),
                                            bc(pre_b[:, c, 4 * g:4 * g + 4], P), ALU.mult)
                    if c < 7:
                        mark(ins)
                ins.then_inc(s_WkS, 1)
            dve.wait_ge(s_WkS, 4)
            dve.wait_ge(s_mkS, 1)
            normalize(Y, T1r)
            link(dve.tensor_tensor(X[:, :, :], X[:, :, :], T1r, ALU.add))
            normalize(X, Y)
            dve.sem_inc(s_rows, 1)

            def ready(u):
                dve.wait_ge(s_sdrain, sbase[u + 1])

            def direct(u):
                t = u // H1
                n = wide(t)
                s_, a_, m_ = S[u % NS][:, 0:n], A[u % NA][:, 0:n], m8[:, u % 2]
                ready(u)
                link(dve.max(m_[:, 0, :], s_))
                if u >= NA:
                    dve.wait_ge(s_tfill, tbase[u - NA] + -(-((u - NA) // H1 + 1) // 4))
                    dve.wait_ge(s_pm, u - NA + 1)
                if u >= 4:
                    dve.wait_ge(s_prob, u - 3)
                mark(dve.tensor_scalar(negm[:, u % 4:u % 4 + 1], m_[:, 0, 0:1], -1.0 / LOW, None, ALU.mult))
                link(dve.match_replace(a_, m_[:, 0, :], s_, -2.0))
                for r in range(1, 8):
                    link(dve.max(m_[:, r, :], a_))
                    if r < 7:
                        link(dve.match_replace(a_, m_[:, r, :], a_, -2.0))
                dve.tensor_scalar(a_, s_, m_[:, 7, 7:8], -2.0, ALU.is_lt, ALU.mult).then_inc(s_keep, 1)

            def normalized(half):
                t, g = divmod(half, 2)
                dve.wait_ge(s_half, half + 1)
                if g == 0 and t:
                    dve.wait_ge(s_tfill, tbase["o", t - 1] + 2)
                link(dve.reciprocal(rden[:, t % 2, 8 * g:8 * g + 8], den[:, t % 2, 8 * g:8 * g + 8]))
                dve.tensor_tensor(O[:, 512 * g:512 * g + 512].rearrange("p (h d) -> p h d", h=8),
                                  bank[6 + g].rearrange("p (h d) -> p h d", h=8),
                                  bc(rden[:, t % 2, 8 * g:8 * g + 8], DH), ALU.mult).then_inc(s_O, 1)

            for s in range(UNITS + 5):
                if s < UNITS:
                    direct(s)
                if s >= 4 and (s - 4) % 8 == 7:
                    normalized((s - 4) // 8)

            dve.wait_ge(s_tdrain, len(pieces))
            dve.wait_ge(s_pm, UNITS)
            normalize(Y, N1)
            link(dve.tensor_tensor(X[:, :, :], X[:, :, :], N1, ALU.add))
            normalize(X, Y)
            normalize(Y, N1)
            dve.wait_ge(s_ln, 48)
            link(dve.tensor_tensor(N1, N1, lnw[:, 0, :].unsqueeze(1).to_broadcast([P, NT, P]), ALU.mult))
            dve.tensor_tensor(N1, N1, lnw[:, 1, :].unsqueeze(1).to_broadcast([P, NT, P]), ALU.add).then_inc(s_rows, 1)
            n = ffills.index("logit1")
            dve.wait_ge(s_ffill, n + 1)
            dve.tensor_copy(L.rearrange("p t e -> p (t e)"), bank[n % 8][:, 0:NT * E0]).then_inc(s_fdrain_v, 1)
            dve.wait_ge(s_fdrain_v, 1)
            first_max(L, sm[:, 4, :], oh1)
            dve.sem_inc(s_sig_in, 1)
            dve.wait_ge(s_sig, 1)
            dve.tensor_tensor(XS, N1, bc(sm[:, 5, :], P), ALU.mult).then_inc(s_rows, 1)

            def ff(name):
                n = ffills.index(name)
                dve.wait_ge(s_ffill, n + 1)
                return bank[n % 8]

            def hidden(n):
                e, b = divmod(n, 4)
                if n >= 4:
                    dve.wait_ge(s_ffill, ffills.index(("d", *divmod(n - 4, 4))) + 1)
                for i in range(2):
                    dve.wait_ge(s_fdrain_a, ffills.drained(ffills.index(("g", e, b, i))))
                    dve.tensor_tensor(hm[:, n % 4, i, :], sg[:, (2 * n + i) % 4, :], ff(("u", e, b, i)), ALU.mult)\
                        .then_inc(s_fdrain_v, 1)

            def gather(n):
                e, b = divmod(n, 4)
                k = ff(("d", e, b))
                if e:
                    dve.wait_ge(s_fdrain_v, ffills.drained(ffills.index(("d", e - 1, b))))
                if e == E0:
                    yb = Y[:, 4 * b:4 * b + 4, :].rearrange("p t c -> p (t c)")
                    dve.tensor_tensor(yb, k, yb, ALU.add).then_inc(s_fdrain_v, 1)
                    return
                for i in range(4):
                    t = 4 * b + i
                    ins = dve.scalar_tensor_tensor(out=Y[:, t, :], in0=k[:, P * i:P * i + P], scalar=oh1[:, t, e:e + 1],
                                                   in1=Y[:, t, :], op0=ALU.mult, op1=ALU.add)
                    if i < 3:
                        mark(ins)
                ins.then_inc(s_fdrain_v, 1)

            hidden(0)
            for n in range(4 * (E0 + 1)):
                if n + 1 < 4 * (E0 + 1):
                    hidden(n + 1)
                gather(n)
            dve.wait_ge(s_dve, done[0])
            dve.wait_ge(s_fdrain_v, ffills.engine.count("dve"))
            normalize(Y, N1)
            dve.tensor_tensor(X[:, :, :], X[:, :, :], N1, ALU.add).then_inc(s_y1, 1)


def kernel(**inputs):
    import numpy as np
    import concourse.bacc as bacc
    from concourse.bass_utils import run_bass_kernel_spmd as run

    nc = bacc.Bacc("TRN2", target_bir_lowering=False, num_devices=1)
    arrays, args = {}, []
    for name in _INS:
        a = np.ascontiguousarray(inputs[name])
        arrays[f"in_{name}"] = a
        args.append(nc.dram_tensor(f"in_{name}", a.shape, mybir.dt.from_np(a.dtype), kind="ExternalInput").ap())
    out = nc.dram_tensor("out", (1, TOK, P), F32, kind="ExternalOutput").ap()
    build(nc, out, *args)
    return run(nc, [arrays], core_ids=[0]).results[0]["out"]
```

```python
from contextlib import ExitStack

import concourse.bass as bass
from concourse import mybir

ALU = mybir.AluOpType
ACT = mybir.ActivationFunctionType
AX = mybir.AxisListType
F32 = mybir.dt.float32

P = 128
TOK = 2048
NT = TOK // P
E0 = 8
FF = 512
H1, DH, MEM, TOPK = 16, 64, 16, 64
INNER = H1 * DH
UNITS = NT * H1
WIDE = MEM + TOK
FI = 256
EPS = 1e-5
LOW = 2.0 ** -30
NS, NA = 5, 4
SC = 1024
BIG_ = 2.0 ** 90
NEAR = 2.0 ** -22
FIRST_FAST = H1
CH = 16
HALF = 2.0 ** 23
CUT = 56

_INS = ['L0_attn_x', 'L0_attn_W_qkv', 'L0_attn_b_qkv', 'L0_ffn_wi', 'L0_ffn_bi', 'L0_ffn_wo', 'L0_ffn_bo',
        'L0_ffn_lora_A', 'L0_ffn_lora_B', 'L0_ffn_gate_w', 'L0_ffn_gate_b', 'L1_attn_Wq', 'L1_attn_Wkv', 'L1_attn_Wo',
        'L1_attn_bo', 'L1_attn_pre_proj', 'L1_attn_mem_k', 'L1_attn_mem_v', 'L1_ffn_ln_w', 'L1_ffn_ln_b',
        'L1_ffn_router_w', 'L1_ffn_gate_w', 'L1_ffn_up_w', 'L1_ffn_down_w', 'L1_ffn_sh_gate', 'L1_ffn_sh_up',
        'L1_ffn_sh_down']


def wide(t):
    return MEM + P * (t + 1)


def slots(t):
    return -(-wide(t) // SC)


class Fills:

    def __init__(self):
        self.names, self.engine = [], []

    def add(self, name, engine):
        self.names.append(name)
        self.engine.append(engine)

    def index(self, name):
        return self.names.index(name)

    def drained(self, n):
        return self.engine[:n + 1].count(self.engine[n])


def plan_fills():
    f = Fills()
    for b in range(4):
        f.add(("h", 0, b), "act")
    for b in range(8):
        f.add(("kv", b), "act")
    for b in range(4):
        f.add(("q", b), "dve")
    f.add("kvsum", "dve")
    for b in range(8):
        f.add(("att", b), "dve")
    for n in ("wi", "wo", "loraB", "loraA_gate"):
        f.add(n, "act")
    for b in range(4):
        f.add(("h", 1, b), "act")
    f.add("logit0", "dve")
    for b in range(4):
        f.add(("lowrank", b), "dve")
    for k in range(2):
        for b in range(4):
            f.add(("pick", k, b), "act")
    for b in range(4):
        for n in range(8):
            f.add(("mid", b, n), "act")
        f.add(("ffn0", b), "dve")
    for b in range(4):
        f.add(("wqk", b), "act")
    f.add("memk", "act")
    f.add("memscore", "act")
    for g in range(4):
        f.add(("G", g), "act")
    for b in range(4):
        f.add(("h", 2, b), "act")
    for t in range(NT):
        for b in range(2):
            f.add(("v", t, b), "act")
    return f


def plan_ffn1():
    f = Fills()
    for b in range(4):
        f.add(("xf", b), "act")
    f.add("logit1", "dve")
    for b in range(4):
        f.add(("xs", b), "act")

    def up(n):
        for i in range(2):
            f.add(("g", *divmod(n, 4), i), "act")
            f.add(("u", *divmod(n, 4), i), "dve")

    up(0)
    for n in range(4 * (E0 + 1)):
        if n + 1 < 4 * (E0 + 1):
            up(n + 1)
        f.add(("d", *divmod(n, 4)), "dve")
    return f


def build(nc, out, x, Wqkv, bqkv, wi, bi, wo, bo0, loraA, loraB, gate_w, gate_b, Wq, Wkv, Wo, bo1, pre, mem_k, mem_v,
          ln_w, ln_b, router_w, gw1, uw1, dw1, shg, shu, shd):
    fills, ffills = plan_fills(), plan_ffn1()
    with ExitStack() as ctx:
        def sb(name, shape, dt=F32):
            return ctx.enter_context(nc.sbuf_tensor(name, shape, dt))

        def sem(name):
            return ctx.enter_context(nc.semaphore(name))

        Xw = sb("Xw", [P, WIDE])
        X = Xw[:, 0:TOK].rearrange("p (t c) -> p t c", t=NT)
        Y = sb("Y", [P, NT, P])
        hT = sb("hT", [P, TOK])
        BIG = sb("BIG", [P, NT * INNER])
        SA = sb("SA", [P, (NS + NA - 1) * WIDE])
        G = sb("G", [P, H1, P])
        Mk = sb("Mk", [P, H1 * MEM])
        qT = sb("qT", [P, H1, P])
        PT = sb("PT", [P, 4, 512])
        Wo_sb = sb("Wo_sb", [P, 8, P])
        mvd = sb("mvd", [P, 2, 512])
        Pm = sb("Pm", [P, H1, MEM])
        PmT = sb("PmT", [P, 2, P])
        O = sb("O", [P, INNER])
        OT = sb("OT", [P, 8, P])
        m8 = sb("m8", [P, 2, 8, 8])
        cand = sb("cand", [P, 2, CH, 8])
        r8 = sb("r8", [P, 2, H1, 8])
        one8 = sb("one8", [P, 8])
        place = sb("place", [P, 8])
        cutb = sb("cutb", [P, 2, H1])
        cutt = sb("cutt", [P, 2])
        cnt = sb("cnt", [P, 2, H1])
        idx = sb("idx", [P, 2, H1])
        thr = sb("thr", [P, 2])
        thrb = sb("thrb", [P, 4])
        tie = sb("tie", [P, 1])
        doubt = sb("doubt", [32, 4])
        doubts = sb("doubts", [32, 2, 32])
        flag = sb("flag", [1, 1], mybir.dt.int32)
        negm = sb("negm", [P, 4])
        den = sb("den", [P, 2, H1])
        rden = sb("rden", [P, 2, H1])
        ident = sb("ident", [P, P])
        cmask = sb("cmask", [P, P])
        onerow = sb("onerow", [1, P])
        tworow = sb("tworow", [1, P])
        rank8 = sb("rank8", [P, NT, E0])
        rows = sb("rows", [1, 256 + E0 + P + P])
        bcol = sb("bcol", [P, 1 + 4])
        st6 = sb("st6", [P, NT, 6])
        mv = sb("mv", [P, NT, 2])
        std = sb("std", [P, NT])
        rstd = sb("rstd", [P, NT])
        sm = sb("sm", [P, 8, NT])
        rt = sb("rt", [P, 4, NT, E0])
        rw_sb = sb("rw_sb", [P, E0])
        gwT = sb("gwT", [P, E0])
        w0 = BIG[:, 12288:16384]
        Wqkv_sb = w0[:, 0:384]
        wiT = w0[:, 384:896]
        woT = w0[:, 896:1408].rearrange("p (f d) -> p f d", f=4)
        lAT = w0[:, 1408:1536]
        lBT = w0[:, 1536:2048]
        kvm = w0[:, 2048:2192]
        ksum = w0[:, 2192:2193]
        bdm = w0[:, 2304:2304 + P]
        kvr = BIG[:, 0:NT * 257].rearrange("p (t c) -> p t c", t=NT)
        pqT = BIG[:, 4112:4112 + TOK]
        pickT = BIG[:, 0:2 * TOK].rearrange("p (k c) -> p k c", k=2)
        mid = BIG[:, 4096:4096 + 8192].rearrange("p (r n c) -> p r n c", r=2, n=8)
        V = BIG[:, :].rearrange("p (t c) -> p t c", t=NT)
        T1 = SA[:, 0:2048]
        T2 = SA[:, 2048:4096]
        pick = SA[:, 0:4096].rearrange("p (k t c) -> p k t c", k=2, t=NT)
        wstage = SA[:, 4096:4096 + 1792]
        wi_r = wstage[:, 0:512].rearrange("p (f c) -> p f c", f=4)
        wo_r = wstage[:, 512:1024]
        lB_r = wstage[:, 1024:1536].rearrange("p (f e r) -> p f e r", f=4, e=E0)
        lA_r = wstage[:, 1536:1664]
        gw_r = wstage[0:E0, 1664:1792]
        Wq_r = SA[:, 6144:7168]
        Wk_r = SA[:, 7168:8192]
        mk_r = SA[0:MEM, 8192:9216]
        Wv_sb = SA[:, 9216:10240]
        pre_b = SA[:, 10240:10368].rearrange("p (c k) -> p c k", c=8)
        WqT = SA[:, 4096:5120].rearrange("p (c n) -> p c n", c=8)
        WkT = SA[:, 5120:6144].rearrange("p (c n) -> p c n", c=8)
        mkT = SA[:, 10368:10496].rearrange("p (c m) -> p c m", c=8)
        mkS = SA[:, 2048:4096].rearrange("p (c k m) -> p c k m", c=8, k=H1)
        S = [SA[:, n * WIDE:(n + 1) * WIDE] for n in range(NS)]
        A = [SA[:, (NS + n) * WIDE:(NS + n + 1) * WIDE] for n in range(NA - 1)] + [Xw[:, :]]
        gw_sb = SA[:, 0:2304].rearrange("p (e i) -> p e i", e=E0 + 1)
        uw_sb = SA[:, 2304:4608].rearrange("p (e i) -> p e i", e=E0 + 1)
        dw_sb = SA[:, 4608:6912].rearrange("p (e i d) -> p e i d", e=E0 + 1, i=2)
        N1 = SA[:, 6912:8960].rearrange("p (t c) -> p t c", t=NT)
        acc = SA[:, 8960:11008].rearrange("p (t c) -> p t c", t=NT)
        xsT = SA[:, 11008:13056]
        lnw = SA[:, 13056:13312].rearrange("p (a c) -> p a c", a=2)
        sg = BIG[:, 0:2048].rearrange("p (r c) -> p r c", r=4)
        hm = BIG[:, 2048:6144].rearrange("p (r i c) -> p r i c", r=4, i=2)
        XS = BIG[:, 6144:8192].rearrange("p (t c) -> p t c", t=NT)
        WkS = BIG[:, 4096:4096 + 8192].rearrange("p (r c k n) -> p r c k n", r=2, c=8, k=4)

        banks = [ctx.enter_context(nc.psum_tensor(f"bank{n}", [P, 2, 512] if n < 4 and n % 2 == 0 else [P, 512], F32))
                 for n in (0, 2, 4, 5, 6, 7)]
        bank = [banks[0][:, 0, :], banks[0][:, 1, :], banks[1][:, 0, :], banks[1][:, 1, :],
                banks[2][:, :], banks[3][:, :], banks[4][:, :], banks[5][:, :]]
        score = [banks[0][:, :, :].rearrange("p a b -> p (a b)"), banks[1][:, :, :].rearrange("p a b -> p (a b)")]

        s_x, s_w0, s_stage, s_wa, s_mv, s_wf, s_ln = (sem(n) for n in
                                                      ("s_x", "s_w0", "s_stage", "s_wa", "s_mv", "s_wf", "s_ln"))
        s_const = sem("s_const")
        s_put, s_got = sem("s_put"), sem("s_got")
        s_dve = sem("s_dve")
        s_act = sem("s_act")
        s_pool = sem("s_pool")
        s_fill = sem("s_fill")
        s_drain_a = sem("s_drain_a")
        s_drain_v = sem("s_drain_v")
        s_rows = sem("s_rows")
        s_var = sem("s_var")
        s_std = sem("s_std")
        s_phi_in, s_phi = sem("s_phi_in"), sem("s_phi")
        s_pk, s_pq = sem("s_pk"), sem("s_pq")
        s_kvm = sem("s_kvm")
        s_logit, s_exp = sem("s_logit"), sem("s_exp")
        s_pick = sem("s_pick")
        s_pre, s_WkS, s_mkS, s_G = sem("s_pre"), sem("s_WkS"), sem("s_mkS"), sem("s_G")
        s_out = sem("s_out")
        s_qfill, s_qT = sem("s_qfill"), sem("s_qT")
        s_sfill, s_sdrain = sem("s_sfill"), sem("s_sdrain")
        s_keep = sem("s_keep")
        s_min = sem("s_min")
        s_cut = sem("s_cut")
        s_over = sem("s_over")
        s_cnt = sem("s_cnt")
        s_below = sem("s_below")
        s_lose = sem("s_lose")
        s_prob = sem("s_prob")
        s_pm = sem("s_pm")
        s_tfill, s_tdrain = sem("s_tfill"), sem("s_tdrain")
        s_pv = sem("s_pv")
        s_scr = sem("s_scr")
        s_half = sem("s_half")
        s_pmT = sem("s_pmT")
        s_O = sem("s_O")
        s_y1 = sem("s_y1")
        s_sig_in, s_sig = sem("s_sig_in"), sem("s_sig")
        s_ffill, s_fdrain_a, s_fdrain_v = (sem(n) for n in ("s_ffill", "s_fdrain_a", "s_fdrain_v"))

        sbase = [0] * (UNITS + 1)
        for u in range(UNITS):
            sbase[u + 1] = sbase[u] + slots(u // H1)
        pieces, tbase = [], {}
        for u in range(UNITS):
            t = u // H1
            tbase[u] = len(pieces)
            pieces += [("p", u, n) for n in range(-(-(t + 1) // 4))]
            if u % 8 == 7:
                tbase["m", u // 8] = len(pieces)
                pieces.append(("m", u // 8, 0))
            for v in ([t - 1] if u % H1 == 3 and t else []) + ([t] if u == UNITS - 1 else []):
                tbase["o", v] = len(pieces)
                pieces += [("o", v, 0), ("o", v, 1), ("y", v, 0)]
        pcount, count = {}, 0
        for n, piece in enumerate(pieces):
            pcount[n] = count
            count += piece[0] == "p"

        block = ctx.enter_context(nc.Block())

        @block.sync
        def _(sp):
            sp.dma_start(X[:, :, :], x[0].rearrange("(t p) c -> p t c", p=P)).then_inc(s_x, 16)
            sp.dma_start(Wqkv_sb, Wqkv).then_inc(s_w0, 16)
            sp.dma_start(wi_r, wi.rearrange("(f p) c -> p f c", p=P)).then_inc(s_stage, 16)
            sp.dma_start(wo_r, wo).then_inc(s_stage, 16)
            for f in range(4):
                sp.dma_start(lB_r[:, f], loraB[:, f * P:(f + 1) * P, :].rearrange("e f r -> f e r")).then_inc(s_stage, 16)
            sp.dma_start(lA_r, loraA.rearrange("e r c -> (e r) c")).then_inc(s_stage, 16)
            sp.dma_start(gw_r, gate_w).then_inc(s_stage, 16)
            sp.wait_ge(s_rows, 3)
            sp.dma_start(out[0].rearrange("(t p) c -> p t c", p=P), X).then_inc(s_put, 16)
            sp.wait_ge(s_put, 16)
            sp.wait_ge(s_tfill, len(pieces))
            sp.wait_ge(s_pm, UNITS)
            sp.dma_start(X, out[0].rearrange("(t p) c -> p t c", p=P)).then_inc(s_got, 16)
            sp.dma_start(lnw[:, 0, :], ln_w.rearrange("(a n) -> a n", a=1).to_broadcast([P, P])).then_inc(s_ln, 16)
            sp.dma_start(lnw[:, 1, :], ln_b.rearrange("(a n) -> a n", a=1).to_broadcast([P, P])).then_inc(s_ln, 16)
            sp.dma_start(gw_sb[:, 0:E0, :], gw1.rearrange("e c i -> c e i")).then_inc(s_wf, 16)
            sp.dma_start(uw_sb[:, 0:E0, :], uw1.rearrange("e c i -> c e i")).then_inc(s_wf, 16)
            sp.dma_start(dw_sb[:, 0:E0], dw1.rearrange("e (i p) d -> p e i d", p=P)).then_inc(s_wf, 16)
            sp.dma_start(gw_sb[:, E0, :], shg).then_inc(s_wf, 16)
            sp.dma_start(uw_sb[:, E0, :], shu).then_inc(s_wf, 16)
            sp.dma_start(dw_sb[:, E0], shd.rearrange("(i p) d -> p i d", p=P)).then_inc(s_wf, 16)
            sp.wait_ge(s_y1, 1)
            sp.dma_start(out[0].rearrange("(t p) c -> p t c", p=P), X[:, :, :]).then_inc(s_out, 16)
            sp.wait_ge(s_out, 16)

        @block.gpsimd
        def _(pool):
            pool.memset(ident[:, :], 0.0).then_inc(s_pool, 1)
            pool.memset(cmask[:, :], 0.0).then_inc(s_pool, 1)
            pool.memset(bdm[:, :], 1.0).then_inc(s_pool, 1)
            pool.memset(onerow[:, :], 1.0).then_inc(s_const, 1)
            pool.memset(tworow[:, :], 2.0).then_inc(s_const, 1)
            pool.memset(kvr[:, :, 256:257], 1.0).then_inc(s_const, 1)
            pool.memset(mvd[:, :, :], 0.0).then_inc(s_pool, 1)
            for n in range(E0):
                pool.memset(rank8[:, :, n:n + 1], float(E0 - n)).then_inc(s_const, 1)
                pool.memset(place[:, n:n + 1], float(n + 1)).then_inc(s_const, 1)
            pool.wait_ge(s_pool, 4)
            pool.affine_select(out=ident[:, :], in_=ident[:, :], compare_op=ALU.not_equal, fill=1.0, base=0,
                               pattern=[[-1, P]], channel_multiplier=1).then_inc(s_const, 1)
            pool.affine_select(out=cmask[:, :], in_=cmask[:, :], compare_op=ALU.is_ge, fill=-1.0, base=0,
                               pattern=[[-1, P]], channel_multiplier=1).then_inc(s_const, 1)
            b3 = bdm[:, :].rearrange("p (b m) -> p b m", b=16)
            pool.affine_select(out=b3, in_=b3, compare_op=ALU.is_ge, fill=0.0, base=0,
                               pattern=[[-8, 16], [0, 8]], channel_multiplier=1).then_inc(s_pool, 1)
            pool.wait_ge(s_pool, 5)
            pool.affine_select(out=b3, in_=b3, compare_op=ALU.is_ge, fill=0.0, base=7,
                               pattern=[[8, 16], [0, 8]], channel_multiplier=-1).then_inc(s_const, 1)
            for h in range(H1):
                pool.dma_start(mvd[MEM * (h % 8):MEM * (h % 8 + 1), h // 8, DH * (h % 8):DH * (h % 8 + 1)],
                               mem_v[h]).then_inc(s_mv, 16)
            for s in range(UNITS + 4):
                if FIRST_FAST <= s - 1 < UNITS:
                    u = s - 1
                    n = wide(u // H1)
                    pool.wait_ge(s_over, u - FIRST_FAST + 1)
                    pool.tensor_tensor(A[u % NA][:, 0:n], S[u % NS][:, 0:n], A[u % NA][:, 0:n], ALU.subtract)\
                        .then_inc(s_below, 1)
                if 2 <= s < UNITS + 2:
                    u = s - 2
                    n = wide(u // H1)
                    if u < FIRST_FAST:
                        pool.wait_ge(s_keep, u + 1)
                    else:
                        pool.wait_ge(s_lose, u - FIRST_FAST + 1)
                    pool.tensor_tensor(A[u % NA][:, 0:n], S[u % NS][:, 0:n], A[u % NA][:, 0:n], ALU.subtract)\
                        .then_inc(s_min, 1)
                if 3 <= s < UNITS + 3:
                    u = s - 3
                    pool.wait_ge(s_prob, u + 1)
                    if u % 8 == 0 and u >= 16:
                        pool.wait_ge(s_tfill, tbase["m", u // 8 - 2] + 1)
                    pool.tensor_copy(Pm[:, u % H1, :], A[u % NA][:, 0:MEM]).then_inc(s_pm, 1)

        @block.scalar
        def _(act):
            acts = [0]

            def link(ins):
                acts[0] += 1
                ins.then_inc(s_act, 1)
                act.wait_ge(s_act, acts[0])

            def drain(name, dst, func=ACT.Copy, src=lambda b: b, **kw):
                n = fills.index(name)
                act.wait_ge(s_fill, n + 1)
                act.activation(dst, src(bank[n % 8]), func, **kw).then_inc(s_drain_a, 1)

            def sqrt(n):
                act.wait_ge(s_var, n)
                act.activation(std[:, :], mv[:, :, 1], ACT.Sqrt).then_inc(s_std, 1)

            act.dma_start(bcol[:, 0:1], bqkv[0:P].rearrange("(p a) -> p a", a=1)).then_inc(s_w0, 16)
            act.dma_start(rows[:, 0:256], bqkv[P:3 * P].rearrange("(a n) -> a n", a=1)).then_inc(s_w0, 16)
            act.dma_start(rows[:, 256:264], gate_b.rearrange("(a n) -> a n", a=1)).then_inc(s_w0, 16)
            act.dma_start(rows[:, 264:392], bo0.rearrange("(a n) -> a n", a=1)).then_inc(s_w0, 16)
            act.dma_start(rows[:, 392:520], bo1.rearrange("(a n) -> a n", a=1)).then_inc(s_w0, 16)
            with nc.allow_non_contiguous_dma(reason="bias by feature"):
                act.dma_start(bcol[:, 1:5], bi.rearrange("(f p) -> p f", p=P)).then_inc(s_w0, 16)
            act.dma_start(rw_sb[:, :], router_w).then_inc(s_ln, 16)
            act.dma_start(Wq_r, Wq).then_inc(s_wa, 16)
            act.dma_start(Wk_r, Wkv[:, 0:INNER]).then_inc(s_wa, 16)
            act.dma_start(Wv_sb, Wkv[:, INNER:2 * INNER]).then_inc(s_wa, 16)
            act.dma_start(mk_r.rearrange("m (h d) -> m h d", h=H1), mem_k.rearrange("h m d -> m h d")).then_inc(s_wa, 16)
            act.dma_start(Wo_sb[:, :, :], Wo.rearrange("(c p) n -> p c n", p=P)).then_inc(s_wa, 16)
            for j in range(2):
                act.dma_start(pre_b[DH * j:DH * (j + 1)],
                              pre.rearrange("(c j) k -> j c k", j=2)[j:j + 1].to_broadcast([DH, 8, H1])).then_inc(s_wa, 16)

            sqrt(1)
            for b in range(4):
                drain(("h", 0, b), hT[:, 512 * b:512 * b + 512])
            for b in range(8):
                drain(("kv", b), kvr[:, 2 * b:2 * b + 2, 0:256], src=lambda k: k.rearrange("p (t c) -> p t c", t=2))
            for n in range(2):
                act.wait_ge(s_phi_in, n + 1)
                act.activation((T1, T2)[n], (T1, T2)[n], ACT.Exp).then_inc(s_phi, 1)
            sqrt(2)
            drain("wi", wiT)
            drain("wo", woT.rearrange("p f d -> p (f d)"))
            drain("loraB", lBT)
            n = fills.index("loraA_gate")
            act.wait_ge(s_fill, n + 1)
            act.activation(lAT, bank[n % 8][:, 0:P], ACT.Copy)
            act.activation(gwT[:, :], bank[n % 8][:, P:P + E0], ACT.Copy).then_inc(s_drain_a, 1)
            sqrt(3)
            for b in range(4):
                drain(("h", 1, b), hT[:, 512 * b:512 * b + 512])
            act.wait_ge(s_logit, 1)
            act.activation(rt[:, 0], rt[:, 0], ACT.Exp).then_inc(s_exp, 1)
            for k in range(2):
                for b in range(4):
                    drain(("pick", k, b), pickT[:, k, 512 * b:512 * b + 512])
            for b in range(4):
                for n in range(8):
                    if n == 0 and b >= 2:
                        act.wait_ge(s_fill, fills.index(("ffn0", b - 2)) + 1)
                    drain(("mid", b, n), mid[:, b % 2, n, :], ACT.Relu, bias=bcol[:, 1 + n % 4:2 + n % 4])
            for b in range(4):
                drain(("wqk", b), (WqT if b < 2 else WkT)[:, 4 * (b % 2):4 * (b % 2) + 4, :].rearrange("p c n -> p (c n)"))
            drain("memk", mkT.rearrange("p c m -> p (c m)"), src=lambda k: k[:, 0:P])
            drain("memscore", Mk[:, :], src=lambda k: k[:, 0:H1 * MEM])
            for g in range(4):
                drain(("G", g), G[:, 4 * g:4 * g + 4, :].rearrange("p k n -> p (k n)"))
            sqrt(4)
            sqrt(5)
            for b in range(4):
                drain(("h", 2, b), hT[:, 512 * b:512 * b + 512])
            for t in range(NT):
                for b in range(2):
                    drain(("v", t, b), V[:, t, 512 * b:512 * b + 512])

            def scores(u):
                t = u // H1
                if u % H1 == 0:
                    for h in range(2):
                        act.wait_ge(s_qfill, 2 * t + h + 1)
                        act.activation(qT[:, 8 * h:8 * h + 8, :].rearrange("p k n -> p (k n)"), score[h], ACT.Copy)\
                            .then_inc(s_qT, 1)
                if u >= NS:
                    act.wait_ge(s_min, u - NS + 1)
                for c in range(slots(t)):
                    w = min(SC, wide(t) - SC * c)
                    act.wait_ge(s_sfill, sbase[u] + c + 1)
                    act.activation(S[u % NS][:, SC * c:SC * c + w], score[(sbase[u] + c) % 2][:, 0:w], ACT.Copy)\
                        .then_inc(s_sdrain, 1)

            def turned(first, count):
                for n in range(first, first + count):
                    kind, v, c = pieces[n]
                    act.wait_ge(s_tfill, n + 1)
                    src = bank[4 + n % 2]
                    if kind == "p":
                        w = min(512, P * (v // H1 + 1) - 512 * c)
                        k = pcount[n]
                        if k >= 4:
                            act.wait_ge(s_pv, k - 3)
                        act.activation(PT[:, k % 4, 0:w], src[:, 0:w], ACT.Copy).then_inc(s_tdrain, 1)
                    elif kind == "m":
                        act.activation(PmT[:, v % 2, :], src[:, 0:P], ACT.Copy).then_inc(s_tdrain, 1)
                    elif kind == "o":
                        act.activation(OT[:, 4 * c:4 * c + 4, :].rearrange("p c n -> p (c n)"), src, ACT.Copy)\
                            .then_inc(s_tdrain, 1)
                    else:
                        act.activation(Y[:, v, :], src[:, 0:P], ACT.Copy).then_inc(s_tdrain, 1)

            for s in range(-2, UNITS + 3):
                u = s - 1
                if FIRST_FAST <= u < UNITS:
                    t, h = divmod(u, H1)
                    n = wide(t)
                    act.wait_ge(s_tfill, tbase[u - NA] + -(-((u - NA) // H1 + 1) // 4))
                    act.wait_ge(s_pm, u - NA + 1)
                    act.wait_ge(s_cut, u - FIRST_FAST + 1)
                    act.activation(A[u % NA][:, 0:n], S[u % NS][:, 0:n], ACT.Sign, bias=cutb[:, t % 2, h:h + 1], scale=BIG_,
                                   accum_out=cnt[:, t % 2, h:h + 1]).then_inc(s_cnt, 1)
                    act.wait_ge(s_cnt, u - FIRST_FAST + 1)
                    act.activation(A[u % NA][:, 0:n], S[u % NS][:, 0:n], ACT.Relu, bias=cutb[:, t % 2, h:h + 1], scale=BIG_)\
                        .then_inc(s_over, 1)
                u = s - 2
                if FIRST_FAST <= u < UNITS:
                    n = wide(u // H1)
                    act.wait_ge(s_keep, u + 1)
                    act.activation(A[u % NA][:, 0:n], S[u % NS][:, 0:n], ACT.Relu, bias=thrb[:, u % 4:u % 4 + 1], scale=-BIG_)\
                        .then_inc(s_lose, 1)
                if s + 2 < UNITS:
                    scores(s + 2)
                u = s - 3
                if 0 <= u < UNITS:
                    n = wide(u // H1)
                    act.wait_ge(s_min, u + 1)
                    act.activation(A[u % NA][:, 0:n], A[u % NA][:, 0:n], ACT.Exp, bias=negm[:, u % 4:u % 4 + 1],
                                   scale=1.0 / LOW, accum_out=den[:, u // H1 % 2, u % H1:u % H1 + 1]).then_inc(s_prob, 1)
                    end = tbase[u + 1] if u + 1 < UNITS else len(pieces)
                    turned(tbase[u], end - tbase[u])

            def fdrain(name, dst, func=ACT.Copy, **kw):
                n = ffills.index(name)
                act.wait_ge(s_ffill, n + 1)
                act.activation(dst, bank[n % 8], func, **kw).then_inc(s_fdrain_a, 1)

            sqrt(6)
            sqrt(7)
            sqrt(8)
            for b in range(4):
                fdrain(("xf", b), hT[:, 512 * b:512 * b + 512])
            act.wait_ge(s_sig_in, 1)
            act.activation(sm[:, 5, :], sm[:, 4, :], ACT.Sigmoid).then_inc(s_sig, 1)
            for b in range(4):
                fdrain(("xs", b), xsT[:, 512 * b:512 * b + 512])
            for e in range(E0 + 1):
                for b in range(4):
                    for i in range(2):
                        k = (e * 4 + b) * 2 + i
                        if k >= 4:
                            m = (k - 4) // 2
                            act.wait_ge(s_fdrain_v, ffills.drained(ffills.index(("u", *divmod(m, 4), k % 2))))
                        fdrain(("g", e, b, i), sg[:, k % 4, :], ACT.Silu)
            sqrt(9)

        @block.tensor
        def _(pe):
            def open_fill(name):
                n = fills.index(name)
                if n >= 8:
                    m = n - 8
                    pe.wait_ge(s_drain_a if fills.engine[m] == "act" else s_drain_v, fills.drained(m))
                return bank[n % 8]

            def turn_rows(which, count, src):
                pe.wait_ge(s_rows, count)
                for b in range(4):
                    k = open_fill((which[0], which[1], b))
                    for i in range(4):
                        last = pe.transpose(k[:, P * i:P * i + P], src[:, 4 * b + i, :], ident[:, :])
                    last.then_inc(s_fill, 1)

            pe.wait_ge(s_const, 3 + 2 * E0 + 3)
            turn_rows(("h", 0), 1, Y)
            pe.wait_ge(s_w0, 16 * 7)
            pe.wait_ge(s_drain_a, 4)
            for b in range(8):
                k = open_fill(("kv", b))
                for i in range(2):
                    t = 2 * b + i
                    pe.matmul(k[:, 256 * i:256 * i + 256], hT[:, P * t:P * t + P], Wqkv_sb[:, P:3 * P], start=True, stop=False)
                    last = pe.matmul(k[:, 256 * i:256 * i + 256], onerow[:, :], rows[:, 0:256], start=False, stop=True)
                last.then_inc(s_fill, 1)
            for b in range(4):
                k = open_fill(("q", b))
                pe.matmul(k, Wqkv_sb[:, 0:P], hT[:, 512 * b:512 * b + 512], start=True, stop=True).then_inc(s_fill, 1)
            pe.wait_ge(s_pk, 1)
            k = open_fill("kvsum")
            for t in range(NT):
                last = pe.matmul(k[:, 0:P + 1], kvr[:, t, 0:P], kvr[:, t, P:257], start=(t == 0), stop=(t == NT - 1))
            last.then_inc(s_fill, 1)
            pe.wait_ge(s_pq, 1)
            pe.wait_ge(s_kvm, 1)
            for b in range(8):
                k = open_fill(("att", b))
                for i in range(2):
                    t = 2 * b + i
                    last = pe.matmul(k[:, 256 * i:256 * i + 144], pqT[:, P * t:P * t + P], kvm, start=True, stop=True)
                last.then_inc(s_fill, 1)
            pe.wait_ge(s_stage, 16 * 8)
            k = open_fill("wi")
            for f in range(4):
                last = pe.transpose(k[:, P * f:P * f + P], wi_r[:, f, :], ident[:, :])
            last.then_inc(s_fill, 1)
            k = open_fill("wo")
            for f in range(4):
                last = pe.transpose(k[:, P * f:P * f + P], wo_r[:, P * f:P * f + P], ident[:, :])
            last.then_inc(s_fill, 1)
            k = open_fill("loraB")
            for f in range(4):
                last = pe.transpose(k[:, P * f:P * f + P], lB_r[:, f].rearrange("p e r -> p (e r)"), ident[:, :])
            last.then_inc(s_fill, 1)
            k = open_fill("loraA_gate")
            pe.transpose(k[:, 0:P], lA_r, ident[:, :])
            pe.transpose(k[:, P:P + E0], gw_r, ident[0:E0, 0:E0]).then_inc(s_fill, 1)
            turn_rows(("h", 1), 2, Y)
            pe.wait_ge(s_drain_a, fills.drained(fills.index(("h", 1, 3))))
            k = open_fill("logit0")
            for t in range(NT):
                pe.matmul(k[:, E0 * t:E0 * t + E0], hT[:, P * t:P * t + P], gwT[:, :], start=True, stop=False)
                last = pe.matmul(k[:, E0 * t:E0 * t + E0], onerow[:, :], rows[:, 256:264], start=False, stop=True)
            last.then_inc(s_fill, 1)
            for b in range(4):
                k = open_fill(("lowrank", b))
                for i in range(4):
                    t = 4 * b + i
                    last = pe.matmul(k[:, P * i:P * i + P], hT[:, P * t:P * t + P], lAT, start=True, stop=True)
                last.then_inc(s_fill, 1)
            for n in range(2):
                pe.wait_ge(s_pick, n + 1)
                for b in range(4):
                    k = open_fill(("pick", n, b))
                    for i in range(4):
                        last = pe.transpose(k[:, P * i:P * i + P], pick[:, n, 4 * b + i, :], ident[:, :])
                    last.then_inc(s_fill, 1)
            pe.wait_ge(s_drain_a, fills.drained(fills.index(("pick", 1, 3))))

            def mids(b):
                for n in range(8):
                    k = open_fill(("mid", b, n))
                    f = n % 4
                    pe.matmul(k, wiT[:, P * f:P * f + P], hT[:, 512 * b:512 * b + 512], start=True, stop=False)
                    pe.matmul(k, lBT[:, P * f:P * f + P], pickT[:, n // 4, 512 * b:512 * b + 512], start=False, stop=True)\
                        .then_inc(s_fill, 1)

            for b in range(4):
                mids(b)
                pe.wait_ge(s_drain_a, fills.drained(fills.index(("mid", b, 7))))
                k = open_fill(("ffn0", b))
                for i in range(4):
                    o = k[:, P * i:P * i + P]
                    for n in range(8):
                        pe.matmul(o, mid[:, b % 2, n, P * i:P * i + P], woT[:, n % 4, :], start=(n == 0), stop=False)
                    last = pe.matmul(o, tworow[:, :], rows[:, 264:392], start=False, stop=True)
                last.then_inc(s_fill, 1)
            pe.wait_ge(s_wa, 16 * 7)
            for b in range(4):
                k = open_fill(("wqk", b))
                for i in range(4):
                    c = 4 * (b % 2) + i
                    last = pe.transpose(k[:, P * i:P * i + P], (Wq_r if b < 2 else Wk_r)[:, P * c:P * c + P], ident[:, :])
                last.then_inc(s_fill, 1)
            k = open_fill("memk")
            for c in range(8):
                last = pe.transpose(k[:, MEM * c:MEM * c + MEM], mk_r[:, P * c:P * c + P], ident[0:MEM, 0:MEM])
            last.then_inc(s_fill, 1)
            k = open_fill("memscore")
            pe.wait_ge(s_mkS, 1)
            for c in range(8):
                last = pe.matmul(k[:, 0:H1 * MEM], WqT[:, c, :], mkS[:, c].rearrange("p k m -> p (k m)"),
                                 start=(c == 0), stop=(c == 7))
            last.then_inc(s_fill, 1)
            for g in range(4):
                k = open_fill(("G", g))
                pe.wait_ge(s_WkS, g + 1)
                for c in range(8):
                    last = pe.matmul(k, WqT[:, c, :], WkS[:, g % 2, c].rearrange("p k n -> p (k n)"),
                                     start=(c == 0), stop=(c == 7))
                last.then_inc(s_fill, 1)
            turn_rows(("h", 2), 3, Y)
            pe.wait_ge(s_drain_a, fills.drained(fills.index(("h", 2, 3))))
            for t in range(NT):
                for b in range(2):
                    k = open_fill(("v", t, b))
                    pe.matmul(k, hT[:, P * t:P * t + P], Wv_sb[:, 512 * b:512 * b + 512], start=True, stop=True)\
                        .then_inc(s_fill, 1)
            pe.wait_ge(s_drain_a, fills.engine.count("act"))
            pe.wait_ge(s_drain_v, fills.engine.count("dve"))
            pe.wait_ge(s_mv, 16 * H1)

            def scores(u):
                t, h = divmod(u, H1)
                if h == 0:
                    if u:
                        pe.wait_ge(s_sdrain, sbase[u])
                    for g in range(2):
                        for i in range(8):
                            last = pe.matmul(score[g][:, P * i:P * i + P], G[:, 8 * g + i, :], hT[:, P * t:P * t + P],
                                             start=True, stop=True)
                        last.then_inc(s_qfill, 1)
                    pe.wait_ge(s_qT, 2 * t + 2)
                n = wide(t)
                for c in range(-(-n // 512)):
                    slot = sbase[u] + c // 2
                    if c % 2 == 0 and slot - 2 >= sbase[u - h]:
                        pe.wait_ge(s_sdrain, slot - 1)
                    a, b = 512 * c, min(512 * c + 512, n)
                    to = score[slot % 2][:, a - SC * (c // 2):b - SC * (c // 2)]
                    d0 = max(a, n - P)
                    masked = d0 < b
                    if c == 0:
                        pe.matmul(to[:, 0:MEM], hT[:, P * t:P * t + P], Mk[:, MEM * h:MEM * h + MEM], start=True, stop=False,
                                  skip_group_check=True)
                        last = pe.matmul(to[:, MEM:], qT[:, h, :], hT[:, 0:b - MEM], start=False, stop=not masked,
                                         skip_group_check=True)
                    else:
                        last = pe.matmul(to, qT[:, h, :], hT[:, a - MEM:b - MEM], start=True, stop=not masked,
                                         skip_group_check=True)
                    if masked:
                        last = pe.matmul(to[:, d0 - a:b - a], ident[:, :], cmask[:, d0 - (n - P):b - (n - P)], start=False,
                                         stop=True, skip_group_check=True)
                    if c % 2 or b == n:
                        last.then_inc(s_sfill, 1)

            def values(u):
                t, h = divmod(u, H1)
                pe.wait_ge(s_prob, u + 1)
                acc_bank = bank[6 + h // 8]
                if h % 8 == 0 and t:
                    pe.wait_ge(s_O, 2 * t - 1 + h // 8)
                n0 = tbase[u]
                np_ = -(-(t + 1) // 4)

                def turn(c):
                    n = n0 + c
                    if n >= 2:
                        pe.wait_ge(s_tdrain, n - 1)
                    blocks = min(4, t + 1 - 4 * c)
                    for i in range(blocks):
                        j = 4 * c + i
                        last = pe.transpose(bank[4 + n % 2][:, P * i:P * i + P],
                                            A[u % NA][:, MEM + P * j:MEM + P * j + P], ident[:, :])
                    last.then_inc(s_tfill, 1)

                def product(c):
                    n = n0 + c
                    pe.wait_ge(s_tdrain, n + 1)
                    blocks = min(4, t + 1 - 4 * c)
                    for i in range(blocks):
                        j = 4 * c + i
                        last = pe.matmul(acc_bank[:, DH * (h % 8):DH * (h % 8) + DH], PT[:, pcount[n] % 4, P * i:P * i + P],
                                         V[:, j, DH * h:DH * h + DH], start=(j == 0 and h % 8 == 0), stop=False,
                                         skip_group_check=True)
                    last.then_inc(s_pv, 1)

                turn(0)
                for c in range(np_):
                    if c + 1 < np_:
                        turn(c + 1)
                    product(c)
                if h % 8 == 7:
                    g = h // 8
                    n = tbase["m", u // 8]
                    pe.wait_ge(s_tdrain, n - 1)
                    pe.wait_ge(s_pm, u + 1)
                    pe.transpose(bank[4 + n % 2][:, 0:P], Pm[:, 8 * g:8 * g + 8, :].rearrange("p h m -> p (h m)"),
                                 ident[:, :]).then_inc(s_tfill, 1)
                    pe.wait_ge(s_tdrain, n + 1)
                    pe.matmul(acc_bank, PmT[:, g, :], mvd[:, g, :], start=False, stop=True, skip_group_check=True)\
                        .then_inc(s_half, 1)
                for v in ([t - 1] if h == 3 and t else []) + ([t] if u == UNITS - 1 else []):
                    n = tbase["o", v]
                    pe.wait_ge(s_O, 2 * v + 2)
                    for g in range(2):
                        pe.wait_ge(s_tdrain, n + g - 1)
                        for i in range(4):
                            last = pe.transpose(bank[4 + (n + g) % 2][:, P * i:P * i + P],
                                                O[:, P * (4 * g + i):P * (4 * g + i) + P], ident[:, :])
                        last.then_inc(s_tfill, 1)
                    pe.wait_ge(s_tdrain, n + 2)
                    y = bank[4 + (n + 2) % 2][:, 0:P]
                    for i in range(8):
                        pe.matmul(y, OT[:, i, :], Wo_sb[:, i, :], start=(i == 0), stop=False)
                    pe.matmul(y, onerow[:, :], rows[:, 392:520], start=False, stop=True).then_inc(s_tfill, 1)

            for s in range(-2, UNITS + 3):
                if s + 2 < UNITS:
                    scores(s + 2)
                if 0 <= s - 3 < UNITS:
                    values(s - 3)

            def open_ffill(name):
                n = ffills.index(name)
                if n >= 8:
                    m = n - 8
                    pe.wait_ge(s_fdrain_a if ffills.engine[m] == "act" else s_fdrain_v, ffills.drained(m))
                return bank[n % 8]

            pe.wait_ge(s_tdrain, len(pieces))
            pe.wait_ge(s_rows, 4)
            for b in range(4):
                k = open_ffill(("xf", b))
                for i in range(4):
                    last = pe.transpose(k[:, P * i:P * i + P], N1[:, 4 * b + i, :], ident[:, :])
                last.then_inc(s_ffill, 1)
            pe.wait_ge(s_fdrain_a, 4)
            pe.wait_ge(s_ln, 48)
            k = open_ffill("logit1")
            for t in range(NT):
                last = pe.matmul(k[:, E0 * t:E0 * t + E0], hT[:, P * t:P * t + P], rw_sb[:, :], start=True, stop=True)
            last.then_inc(s_ffill, 1)
            pe.wait_ge(s_rows, 5)
            for b in range(4):
                k = open_ffill(("xs", b))
                for i in range(4):
                    last = pe.transpose(k[:, P * i:P * i + P], XS[:, 4 * b + i, :], ident[:, :])
                last.then_inc(s_ffill, 1)
            pe.wait_ge(s_fdrain_a, 8)
            pe.wait_ge(s_wf, 16 * 6)

            def up(n):
                e, b = divmod(n, 4)
                src = (xsT if e < E0 else hT[:, :])[:, 512 * b:512 * b + 512]
                for i in range(2):
                    for kind, w in (("g", gw_sb), ("u", uw_sb)):
                        k = open_ffill((kind, e, b, i))
                        pe.matmul(k, w[:, e, P * i:P * i + P], src, start=True, stop=True).then_inc(s_ffill, 1)

            def down(n):
                e, b = divmod(n, 4)
                pe.wait_ge(s_fdrain_v, ffills.drained(ffills.index(("u", e, b, 1))))
                k = open_ffill(("d", e, b))
                for i in range(4):
                    for c in range(2):
                        last = pe.matmul(k[:, P * i:P * i + P], hm[:, n % 4, c, P * i:P * i + P], dw_sb[:, e, c, :],
                                         start=(c == 0), stop=(c == 1))
                last.then_inc(s_ffill, 1)

            up(0)
            for n in range(4 * (E0 + 1)):
                if n + 1 < 4 * (E0 + 1):
                    up(n + 1)
                down(n)

        @block.vector
        def _(dve):
            done = [0]

            def mark(ins):
                done[0] += 1
                ins.then_inc(s_dve, 1)

            def link(ins):
                mark(ins)
                dve.wait_ge(s_dve, done[0])

            norms = [0]

            def normalize(src, dst):
                norms[0] += 1
                for t in range(NT):
                    mark(dve.bn_stats(st6[:, t, :], src[:, t, :]))
                dve.wait_ge(s_dve, done[0])
                for t in range(NT):
                    mark(dve.bn_aggr(mv[:, t, :], st6[:, t, :]))
                dve.wait_ge(s_dve, done[0])
                dve.tensor_scalar(mv[:, :, 1], mv[:, :, 1], EPS, None, ALU.add).then_inc(s_var, 1)
                dve.wait_ge(s_std, norms[0])
                link(dve.reciprocal(rstd[:, :], std[:, :]))
                for t in range(NT):
                    mark(dve.tensor_scalar(dst[:, t, :], src[:, t, :], mv[:, t, 0:1], rstd[:, t:t + 1],
                                           ALU.subtract, ALU.mult))
                dve.wait_ge(s_dve, done[0])

            def drained(name):
                n = fills.index(name)
                dve.wait_ge(s_fill, n + 1)
                return bank[n % 8]

            def bc(ap, n):
                return ap.unsqueeze(len(ap.shape)).to_broadcast(list(ap.shape) + [n])

            T1r = T1.rearrange("p (t c) -> p t c", t=NT)

            dve.wait_ge(s_x, 16)
            normalize(X, Y)
            dve.sem_inc(s_rows, 1)
            for b in range(4):
                k = drained(("q", b))
                dve.tensor_scalar(pqT[:, 512 * b:512 * b + 512], k, bcol[:, 0:1], None, ALU.add).then_inc(s_drain_v, 1)
            keys = kvr[:, :, 0:P]
            dve.wait_ge(s_drain_a, fills.drained(fills.index(("kv", 7))))
            dve.tensor_scalar(T1r, keys, 0.0, None, ALU.min).then_inc(s_phi_in, 1)
            dve.wait_ge(s_drain_v, 4)
            dve.tensor_scalar(T2, pqT, 0.0, None, ALU.min).then_inc(s_phi_in, 1)
            dve.wait_ge(s_phi, 1)
            dve.scalar_tensor_tensor(out=keys, in0=keys, scalar=0.0, in1=T1r, op0=ALU.max, op1=ALU.add).then_inc(s_pk, 1)
            dve.wait_ge(s_phi, 2)
            dve.scalar_tensor_tensor(out=pqT, in0=pqT, scalar=0.0, in1=T2, op0=ALU.max, op1=ALU.add).then_inc(s_pq, 1)
            k = drained("kvsum")
            dve.wait_ge(s_const, 3 + 2 * E0 + 3)
            mark(dve.tensor_tensor(kvm[:, 0:P], k[:, 0:P], bdm[:, :], ALU.mult))
            dve.tensor_copy(ksum, k[:, P:P + 1]).then_inc(s_drain_v, 1)
            dve.wait_ge(s_drain_v, 5)
            dve.wait_ge(s_dve, done[0])
            dve.tensor_scalar(kvm[:, P:P + 16], bdm[:, :].rearrange("p (b m) -> p b m", b=16)[:, :, 0], ksum, None,
                              ALU.mult).then_inc(s_kvm, 1)
            for b in range(8):
                k = drained(("att", b)).rearrange("p (t c) -> p t c", t=2)
                d = sm[:, 0:4, :].rearrange("p a t -> p (a t)")[:, 0:32].rearrange("p (t h) -> p t h", t=2)
                link(dve.tensor_scalar(d, k[:, :, P:P + 16], 1e-6, None, ALU.add))
                link(dve.reciprocal(d, d))
                dve.tensor_tensor(Y[:, 2 * b:2 * b + 2, :].rearrange("p t (h m) -> p t h m", h=16),
                                  k[:, :, 0:P].rearrange("p t (h m) -> p t h m", h=16), bc(d, 8), ALU.mult)\
                    .then_inc(s_drain_v, 1)
                dve.wait_ge(s_drain_v, 6 + b)
            normalize(Y, T1r)
            link(dve.tensor_tensor(X[:, :, :], X[:, :, :], T1r, ALU.add))
            normalize(X, Y)
            dve.sem_inc(s_rows, 1)
            k = drained("logit0")
            L, oh1, oh2, tmp = rt[:, 0], rt[:, 1], rt[:, 2], rt[:, 3]
            dve.tensor_copy(L.rearrange("p t e -> p (t e)"), k[:, 0:NT * E0]).then_inc(s_drain_v, 1)
            dve.wait_ge(s_drain_v, fills.drained(fills.index("logit0")))
            link(dve.tensor_reduce(sm[:, 0, :], L, AX.X, ALU.max))
            dve.tensor_tensor(L, L, bc(sm[:, 0, :], E0), ALU.subtract).then_inc(s_logit, 1)
            dve.wait_ge(s_exp, 1)
            link(dve.tensor_reduce(sm[:, 1, :], L, AX.X, ALU.add))
            dve.wait_ge(s_const, 3 + 2 * E0 + 3)

            def first_max(values, best, onehot):
                link(dve.tensor_reduce(best, values, AX.X, ALU.max))
                link(dve.tensor_tensor(tmp, values, bc(best, E0), ALU.is_equal))
                link(dve.tensor_tensor(tmp, tmp, rank8[:, :, :], ALU.mult))
                link(dve.tensor_reduce(sm[:, 7, :], tmp, AX.X, ALU.max))
                link(dve.tensor_tensor(onehot, tmp, bc(sm[:, 7, :], E0), ALU.is_equal))

            first_max(L, sm[:, 2, :], oh1)
            link(dve.scalar_tensor_tensor(out=L, in0=oh1, scalar=-2.0, in1=L, op0=ALU.mult, op1=ALU.add))
            first_max(L, sm[:, 3, :], oh2)
            link(dve.tensor_tensor(sm[:, 2, :], sm[:, 2, :], sm[:, 3, :], ALU.add))
            link(dve.reciprocal(sm[:, 1, :], sm[:, 1, :]))
            link(dve.tensor_tensor(sm[:, 2, :], sm[:, 2, :], sm[:, 1, :], ALU.mult))
            for n in range(2):
                for b in range(4):
                    k = drained(("lowrank", b)).rearrange("p (t e r) -> p t e r", t=4, e=E0)
                    ins = dve.tensor_tensor(pick[:, n, 4 * b:4 * b + 4, :].rearrange("p t (e r) -> p t e r", e=E0), k,
                                            bc((oh1, oh2)[n][:, 4 * b:4 * b + 4, :], MEM), ALU.mult)
                    if n == 1:
                        ins.then_inc(s_drain_v, 1)
                    else:
                        mark(ins)
                dve.wait_ge(s_dve, done[0])
                if n:
                    dve.wait_ge(s_drain_v, fills.drained(fills.index(("lowrank", 3))))
                dve.sem_inc(s_pick, 1)
            for b in range(4):
                k = drained(("ffn0", b))
                for i in range(4):
                    t = 4 * b + i
                    ins = dve.tensor_scalar(Y[:, t, :], k[:, P * i:P * i + P], sm[:, 2, t:t + 1], None, ALU.mult)
                    if i < 3:
                        mark(ins)
                ins.then_inc(s_drain_v, 1)
                if b == 1:
                    dve.wait_ge(s_wa, 16 * 7)
                    link(dve.tensor_scalar(pre_b, pre_b, DH ** -0.5 * LOW, None, ALU.mult))
            dve.wait_ge(s_dve, done[0])
            dve.wait_ge(s_drain_v, fills.drained(fills.index(("ffn0", 3))))
            dve.wait_ge(s_drain_a, fills.drained(fills.index("memk")))
            dve.tensor_tensor(mkS, mkT.unsqueeze(2).to_broadcast([P, 8, H1, MEM]), bc(pre_b, MEM), ALU.mult)\
                .then_inc(s_mkS, 1)
            for g in range(4):
                if g >= 2:
                    dve.wait_ge(s_fill, fills.index(("G", g - 2)) + 1)
                for c in range(8):
                    ins = dve.tensor_tensor(WkS[:, g % 2, c], WkT[:, c, :].unsqueeze(1).to_broadcast([P, 4, P]),
                                            bc(pre_b[:, c, 4 * g:4 * g + 4], P), ALU.mult)
                    if c < 7:
                        mark(ins)
                ins.then_inc(s_WkS, 1)
            dve.wait_ge(s_WkS, 4)
            dve.wait_ge(s_mkS, 1)
            normalize(Y, T1r)
            link(dve.tensor_tensor(X[:, :, :], X[:, :, :], T1r, ALU.add))
            normalize(X, Y)
            dve.sem_inc(s_rows, 1)

            def direct(u):
                t = u // H1
                n = wide(t)
                s_, a_, m_ = S[u % NS][:, 0:n], A[u % NA][:, 0:n], m8[:, u % 2]
                dve.wait_ge(s_sdrain, sbase[u + 1])
                link(dve.max(m_[:, 0, :], s_))
                if u == NA - 1:
                    dve.wait_ge(s_put, 16)
                if u >= NA:
                    dve.wait_ge(s_tfill, tbase[u - NA] + -(-((u - NA) // H1 + 1) // 4))
                    dve.wait_ge(s_pm, u - NA + 1)
                if u >= 4:
                    dve.wait_ge(s_prob, u - 3)
                mark(dve.tensor_scalar(negm[:, u % 4:u % 4 + 1], m_[:, 0, 0:1], -1.0 / LOW, None, ALU.mult))
                link(dve.match_replace(a_, m_[:, 0, :], s_, -2.0))
                for r in range(1, 8):
                    link(dve.max(m_[:, r, :], a_))
                    if r < 7:
                        link(dve.match_replace(a_, m_[:, r, :], a_, -2.0))
                dve.tensor_scalar(a_, s_, m_[:, 7, 7:8], 2.0, ALU.is_lt, ALU.mult).then_inc(s_keep, 1)

            def normalized(half):
                t, g = divmod(half, 2)
                dve.wait_ge(s_half, half + 1)
                if g == 0 and t:
                    dve.wait_ge(s_tfill, tbase["o", t - 1] + 2)
                link(dve.reciprocal(rden[:, t % 2, 8 * g:8 * g + 8], den[:, t % 2, 8 * g:8 * g + 8]))
                dve.tensor_tensor(O[:, 512 * g:512 * g + 512].rearrange("p (h d) -> p h d", h=8),
                                  bank[6 + g].rearrange("p (h d) -> p h d", h=8),
                                  bc(rden[:, t % 2, 8 * g:8 * g + 8], DH), ALU.mult).then_inc(s_O, 1)

            def chunk(u, c):
                t = u // H1
                if c == 0:
                    dve.wait_ge(s_sdrain, sbase[u + 1])
                ins = dve.max(cand[:, u % 2, c, :], S[u % NS][:, c:wide(t):CH])
                if c == CH - 1:
                    mark(ins)
                    chunks_done[u] = done[0]

            def below(u):
                t, h = divmod(u, H1)
                n = wide(t)
                dve.wait_ge(s_cnt, u - FIRST_FAST + 1)
                mark(dve.tensor_scalar(cutt[:, u % 2:u % 2 + 1], cnt[:, t % 2, h:h + 1], -0.5, TOPK - n / 2 + 0.25,
                                       ALU.mult, ALU.add))
                at = done[0]
                dve.wait_ge(s_below, u - FIRST_FAST + 1)
                mark(dve.max(r8[:, t % 2, h, :], A[u % NA][:, 0:n]))
                dve.wait_ge(s_dve, at)
                mark(dve.tensor_scalar(idx[:, t % 2, h:h + 1], cutt[:, u % 2:u % 2 + 1], HALF, -HALF, ALU.add, ALU.add))
                below_done[u] = done[0]

            def pick_threshold(u):
                t, h = divmod(u, H1)
                dve.wait_ge(s_dve, below_done[u])
                mark(dve.scalar_tensor_tensor(out=one8[:, :], in0=place[:, :], scalar=idx[:, t % 2, h:h + 1],
                                              in1=r8[:, t % 2, h, :], op0=ALU.is_equal, op1=ALU.mult,
                                              accum_out=thr[:, u % 2:u % 2 + 1]))
                mark(dve.scalar_tensor_tensor(out=tie[:, :], in0=r8[:, t % 2, h, 1:2], scalar=-BIG_,
                                              in1=cutb[:, t % 2, h:h + 1], op0=ALU.mult, op1=ALU.is_le))
                thr_done[u] = done[0]

            def scale_threshold(u):
                dve.wait_ge(s_dve, thr_done[u])
                if u >= FIRST_FAST + 4:
                    dve.wait_ge(s_lose, u - FIRST_FAST - 3)
                dve.tensor_scalar(thrb[:, u % 4:u % 4 + 1], thr[:, u % 2:u % 2 + 1], BIG_, None, ALU.mult)\
                    .then_inc(s_keep, 1)

            def doubt_rows(u):
                dve.wait_ge(s_dve, thr_done[u])
                for g in range(4):
                    rows_g = slice(32 * g, 32 * g + 32)
                    mark(dve.scalar_tensor_tensor(out=doubt[:, g:g + 1], in0=thr[rows_g, u % 2:u % 2 + 1], scalar=0.0,
                                                  in1=tie[rows_g, :], op0=ALU.is_equal, op1=ALU.max))
                thr_done[u] = done[0]

            def doubt_max(u):
                dve.wait_ge(s_dve, thr_done[u])
                mark(dve.tensor_reduce(doubts[:, 0, 0:1], doubt[:, :], AX.X, ALU.max))
                thr_done[u] = done[0]

            def doubt_turn(u):
                dve.wait_ge(s_dve, thr_done[u])
                mark(dve.transpose(doubts[:, 1, :], doubts[:, 0, :]))
                thr_done[u] = done[0]

            def doubt_any(u):
                dve.wait_ge(s_dve, thr_done[u])
                mark(dve.tensor_reduce(flag[:, :], doubts[0:1, 1, :], AX.X, ALU.max))
                thr_done[u] = done[0]

            def settle(u):
                t, h = divmod(u, H1)
                n = wide(t)
                s_, a_, m_ = S[u % NS][:, 0:n], A[u % NA][:, 0:n], r8[:, t % 2, h, :]
                dve.wait_ge(s_dve, thr_done[u])
                doubtful = dve.value_load(flag[0:1, 0:1], min_val=0, max_val=1)
                with dve.If(doubtful != 0):
                    for r in range(8):
                        dve.max(m_, a_ if r else s_)
                        dve.drain()
                        if r < 7:
                            dve.match_replace(a_, m_, a_ if r else s_, -2.0)
                            dve.drain()
                    dve.tensor_copy(thr[:, u % 2:u % 2 + 1], m_[:, 7:8])
                    dve.drain()

            steps = (doubt_rows, doubt_max, doubt_turn, doubt_any, settle)

            def fast(u):
                t, h = divmod(u, H1)
                m_, c_ = m8[:, u % 2], cand[:, u % 2].rearrange("p c e -> p (c e)")
                more = u + 1 < UNITS
                dve.wait_ge(s_dve, chunks_done[u])
                for r in range(CUT // 8):
                    mark(dve.max(m_[:, r, :], c_))
                    at = done[0]
                    if more:
                        chunk(u + 1, 2 * r)
                    if r == 0:
                        dve.wait_ge(s_dve, at)
                        if u >= 4:
                            dve.wait_ge(s_prob, u - 3)
                        mark(dve.tensor_scalar(negm[:, u % 4:u % 4 + 1], m_[:, 0, 0:1], -1.0 / LOW, None, ALU.mult))
                        if u - 2 >= FIRST_FAST:
                            pick_threshold(u - 2)
                    if 1 <= r <= 2 and u - 2 >= FIRST_FAST:
                        steps[2 * r - 1](u - 2)
                    if r == 3 and u - 2 >= FIRST_FAST:
                        settle(u - 2)
                        scale_threshold(u - 2)
                    dve.wait_ge(s_dve, at)
                    if r < CUT // 8 - 1:
                        mark(dve.match_replace(c_, m_[:, r, :], c_, -2.0))
                        at = done[0]
                        if more:
                            chunk(u + 1, 2 * r + 1)
                        if r <= 1 and u - 2 >= FIRST_FAST:
                            steps[2 * r](u - 2)
                        dve.wait_ge(s_dve, at)
                v = m_[:, CUT // 8 - 1, 7:8]
                mark(dve.tensor_scalar(cutt[:, u % 2:u % 2 + 1], v, -BIG_ * (1 - NEAR), None, ALU.mult))
                at = done[0]
                if more:
                    chunk(u + 1, 13)
                dve.wait_ge(s_dve, at)
                dve.scalar_tensor_tensor(out=cutb[:, t % 2, h:h + 1], in0=v, scalar=-BIG_ * (1 + NEAR),
                                         in1=cutt[:, u % 2:u % 2 + 1], op0=ALU.mult, op1=ALU.max).then_inc(s_cut, 1)
                if more:
                    chunk(u + 1, 14)
                    chunk(u + 1, 15)

            chunks_done, below_done, thr_done = {}, {}, {}
            link(dve.memset(doubts[:, :, :], 0.0))
            for s in range(UNITS + 5):
                if s < FIRST_FAST:
                    direct(s)
                    if s + 1 == FIRST_FAST:
                        for c in range(CH):
                            chunk(s + 1, c)
                elif s < UNITS:
                    fast(s)
                elif s - 2 < UNITS:
                    pick_threshold(s - 2)
                    for step in steps:
                        step(s - 2)
                    scale_threshold(s - 2)
                if FIRST_FAST <= s - 1 < UNITS:
                    below(s - 1)
                if s >= 4 and (s - 4) % 8 == 7:
                    normalized((s - 4) // 8)

            dve.wait_ge(s_tdrain, len(pieces))
            dve.wait_ge(s_pm, UNITS)
            normalize(Y, N1)
            dve.wait_ge(s_got, 16)
            link(dve.tensor_tensor(X[:, :, :], X[:, :, :], N1, ALU.add))
            normalize(X, Y)
            normalize(Y, N1)
            dve.wait_ge(s_ln, 48)
            link(dve.tensor_tensor(N1, N1, lnw[:, 0, :].unsqueeze(1).to_broadcast([P, NT, P]), ALU.mult))
            dve.tensor_tensor(N1, N1, lnw[:, 1, :].unsqueeze(1).to_broadcast([P, NT, P]), ALU.add).then_inc(s_rows, 1)
            n = ffills.index("logit1")
            dve.wait_ge(s_ffill, n + 1)
            dve.tensor_copy(L.rearrange("p t e -> p (t e)"), bank[n % 8][:, 0:NT * E0]).then_inc(s_fdrain_v, 1)
            dve.wait_ge(s_fdrain_v, 1)
            first_max(L, sm[:, 4, :], oh1)
            dve.sem_inc(s_sig_in, 1)
            dve.wait_ge(s_sig, 1)
            dve.tensor_tensor(XS, N1, bc(sm[:, 5, :], P), ALU.mult).then_inc(s_rows, 1)

            def ff(name):
                n = ffills.index(name)
                dve.wait_ge(s_ffill, n + 1)
                return bank[n % 8]

            def hidden(n):
                e, b = divmod(n, 4)
                if n >= 4:
                    dve.wait_ge(s_ffill, ffills.index(("d", *divmod(n - 4, 4))) + 1)
                for i in range(2):
                    dve.wait_ge(s_fdrain_a, ffills.drained(ffills.index(("g", e, b, i))))
                    dve.tensor_tensor(hm[:, n % 4, i, :], sg[:, (2 * n + i) % 4, :], ff(("u", e, b, i)), ALU.mult)\
                        .then_inc(s_fdrain_v, 1)

            def gather(n):
                e, b = divmod(n, 4)
                k = ff(("d", e, b))
                if e:
                    dve.wait_ge(s_fdrain_v, ffills.drained(ffills.index(("d", e - 1, b))))
                if e == E0:
                    yb = Y[:, 4 * b:4 * b + 4, :].rearrange("p t c -> p (t c)")
                    dve.tensor_tensor(yb, k, yb, ALU.add).then_inc(s_fdrain_v, 1)
                    return
                for i in range(4):
                    t = 4 * b + i
                    ins = dve.scalar_tensor_tensor(out=Y[:, t, :], in0=k[:, P * i:P * i + P], scalar=oh1[:, t, e:e + 1],
                                                   in1=Y[:, t, :], op0=ALU.mult, op1=ALU.add)
                    if i < 3:
                        mark(ins)
                ins.then_inc(s_fdrain_v, 1)

            hidden(0)
            for n in range(4 * (E0 + 1)):
                if n + 1 < 4 * (E0 + 1):
                    hidden(n + 1)
                gather(n)
            dve.wait_ge(s_dve, done[0])
            dve.wait_ge(s_fdrain_v, ffills.engine.count("dve"))
            normalize(Y, N1)
            dve.tensor_tensor(X[:, :, :], X[:, :, :], N1, ALU.add).then_inc(s_y1, 1)


def kernel(**inputs):
    import numpy as np
    import concourse.bacc as bacc
    from concourse.bass_utils import run_bass_kernel_spmd as run

    nc = bacc.Bacc("TRN2", target_bir_lowering=False, num_devices=1)
    arrays, args = {}, []
    for name in _INS:
        a = np.ascontiguousarray(inputs[name])
        arrays[f"in_{name}"] = a
        args.append(nc.dram_tensor(f"in_{name}", a.shape, mybir.dt.from_np(a.dtype), kind="ExternalInput").ap())
    out = nc.dram_tensor("out", (1, TOK, P), F32, kind="ExternalOutput").ap()
    build(nc, out, *args)
    return run(nc, [arrays], core_ids=[0]).results[0]["out"]
```
